# Optimizing a Trainium2 kernel written in Bass

```python
import numpy as np
import jax
import jax.numpy as jnp

def _softmax(x, axis=-1):
    return jax.nn.softmax(x, axis=axis)

def _gelu(x):
    return jax.nn.gelu(x, approximate=True)

def _silu(x):
    return jax.nn.silu(x)

def _sigmoid(x):
    return jax.nn.sigmoid(x)

def _layernorm(x, axis=-1, eps=1e-05):
    m = jnp.mean(x, axis=axis, keepdims=True)
    v = jnp.var(x, axis=axis, keepdims=True)
    return (x - m) / jnp.sqrt(v + eps)

def _scatter_add(tgt, idx, src, axis=0):
    return tgt.at[idx].add(src)

def _segment_sum(src, seg, n):
    return jax.ops.segment_sum(src, seg, n)
kernel_name = 'mk_gnn_resnorm_d2_gnn_r8_3d6af7'

def setup_inputs(seed: int=0):
    np.random.seed(seed)
    _w = jnp.asarray

    def _rec_inputs():
        import jax
        import jax.numpy as jnp
        _gk = jax.random.key(seed)
        x = -0.0003713 + 1 * jax.random.normal(jax.random.fold_in(_gk, 1), (12500, 128), jnp.float32)
        src = jax.random.randint(jax.random.fold_in(_gk, 2), (400000,), 0, 12500, jnp.int32)
        dst = jax.random.randint(jax.random.fold_in(_gk, 3), (400000,), 0, 12500, jnp.int32)
        _o = jnp.argsort(dst, stable=True)
        src = src[_o]
        dst = dst[_o]
        edge_attr_64 = 0.000167468 + 1.0002 * jax.random.normal(jax.random.fold_in(_gk, 11), (400000, 64), jnp.float32)
        return (x, src, dst, edge_attr_64)
    x, src, dst, edge_attr_64 = _rec_inputs()

    def _L0_gnn_setup():
        import jax, jax.numpy as jnp
        import numpy as np
        N_NODES = 12500
        N_EDGES = 200000
        D = 128
        key = jax.random.key(seed)
        ks = jax.random.split(key, 6)
        x = jax.random.normal(ks[0], (N_NODES, D), dtype=jnp.float32)
        edge_index = jax.random.randint(ks[1], (2, N_EDGES), 0, N_NODES, dtype=jnp.int64)
        eps = jnp.zeros((1,), dtype=jnp.float32)
        scale = 1.0 / np.sqrt(D)
        W1 = jax.random.normal(ks[2], (D, D), dtype=jnp.float32) * scale
        b1 = jnp.zeros((D,), dtype=jnp.float32)
        W2 = jax.random.normal(ks[3], (D, D), dtype=jnp.float32) * scale
        b2 = jnp.zeros((D,), dtype=jnp.float32)
        return {'x': x, 'edge_index': edge_index, 'eps': eps, 'W1': W1, 'b1': b1, 'W2': W2, 'b2': b2}
    _L0_gnn_all = _L0_gnn_setup()
    _L0_gnn_in = {k: v for k, v in _L0_gnn_all.items() if k in ('eps', 'W1', 'b1', 'W2', 'b2')}
    del _L0_gnn_all

    def _L1_gnn_setup():
        import jax, jax.numpy as jnp
        import numpy as np
        N = 5000
        E = 80000
        ND = 128
        ED = 64
        LN_EPS = 1e-05
        key = jax.random.key(seed)
        ks = jax.random.split(key, 16)
        s = lambda k, shape, fan_in: jax.random.normal(k, shape, dtype=jnp.float32) * (1.0 / np.sqrt(fan_in))
        return {'node_features': jax.random.normal(ks[0], (N, ND), dtype=jnp.float32), 'edge_indices': jax.random.randint(ks[1], (2, E), 0, N, dtype=jnp.int32), 'edge_features': jax.random.normal(ks[2], (E, ED), dtype=jnp.float32), 'W1': s(ks[3], (2 * ND + ED, ND), 2 * ND + ED), 'b1': jnp.zeros((ND,), jnp.float32), 'ln_g': jnp.ones((ND,), jnp.float32), 'ln_b': jnp.zeros((ND,), jnp.float32), 'W2': s(ks[4], (ND, ND), ND), 'b2': jnp.zeros((ND,), jnp.float32), 'gate_w': s(ks[5], (ED, 1), ED), 'gate_b': jnp.zeros((1,), jnp.float32), 'W_ih': s(ks[6], (3 * ND, ND), ND), 'b_ih': jnp.zeros((3 * ND,), jnp.float32), 'W_hh': s(ks[7], (3 * ND, ND), ND), 'b_hh': jnp.zeros((3 * ND,), jnp.float32)}
    _L1_gnn_all = _L1_gnn_setup()
    _L1_gnn_in = {k: v for k, v in _L1_gnn_all.items() if k in ('W1', 'b1', 'ln_g', 'ln_b', 'W2', 'b2', 'gate_w', 'gate_b', 'W_ih', 'b_ih', 'W_hh', 'b_hh')}
    del _L1_gnn_all
    return {'x': x, 'src': src, 'dst': dst, 'edge_attr_64': edge_attr_64, 'L0_gnn_eps': _L0_gnn_in['eps'], 'L0_gnn_W1': _L0_gnn_in['W1'], 'L0_gnn_b1': _L0_gnn_in['b1'], 'L0_gnn_W2': _L0_gnn_in['W2'], 'L0_gnn_b2': _L0_gnn_in['b2'], 'L1_gnn_W1': _L1_gnn_in['W1'], 'L1_gnn_b1': _L1_gnn_in['b1'], 'L1_gnn_ln_g': _L1_gnn_in['ln_g'], 'L1_gnn_ln_b': _L1_gnn_in['ln_b'], 'L1_gnn_W2': _L1_gnn_in['W2'], 'L1_gnn_b2': _L1_gnn_in['b2'], 'L1_gnn_gate_w': _L1_gnn_in['gate_w'], 'L1_gnn_gate_b': _L1_gnn_in['gate_b'], 'L1_gnn_W_ih': _L1_gnn_in['W_ih'], 'L1_gnn_b_ih': _L1_gnn_in['b_ih'], 'L1_gnn_W_hh': _L1_gnn_in['W_hh'], 'L1_gnn_b_hh': _L1_gnn_in['b_hh']}

def reference(x, src, dst, edge_attr_64, L0_gnn_eps, L0_gnn_W1, L0_gnn_b1, L0_gnn_W2, L0_gnn_b2, L1_gnn_W1, L1_gnn_b1, L1_gnn_ln_g, L1_gnn_ln_b, L1_gnn_W2, L1_gnn_b2, L1_gnn_gate_w, L1_gnn_gate_b, L1_gnn_W_ih, L1_gnn_b_ih, L1_gnn_W_hh, L1_gnn_b_hh):
    import jax
    import jax.numpy as jnp

    def _L0_gnn_ref(x, edge_index, eps, W1, b1, W2, b2):
        import jax, jax.numpy as jnp
        import numpy as np
        N_NODES = 12500
        N_EDGES = 200000
        D = 128
        src, dst = (edge_index[0], edge_index[1])
        agg = jax.ops.segment_sum(x[src], dst, num_segments=N_NODES)
        y = agg + (1.0 + eps[0]) * x
        h = jax.nn.relu(y @ W1 + b1)
        out = h @ W2 + b2
        return out

    def _L1_gnn_ref(node_features, edge_indices, edge_features, W1, b1, ln_g, ln_b, W2, b2, gate_w, gate_b, W_ih, b_ih, W_hh, b_hh):
        import jax, jax.numpy as jnp
        import numpy as np
        N = 5000
        E = 80000
        ND = 128
        ED = 64
        LN_EPS = 1e-05
        src, dst = (edge_indices[0], edge_indices[1])
        edge_inputs = jnp.concatenate([node_features[src], node_features[dst], edge_features], axis=1)
        h = edge_inputs @ W1 + b1
        mu = jnp.mean(h, axis=-1, keepdims=True)
        var = jnp.var(h, axis=-1, keepdims=True)
        h = (h - mu) * jax.lax.rsqrt(var + LN_EPS) * ln_g + ln_b
        h = jax.nn.relu(h)
        messages = h @ W2 + b2
        gate = jax.nn.sigmoid(edge_features @ gate_w + gate_b)
        messages = messages * gate
        agg = jax.ops.segment_sum(messages, dst, num_segments=node_features.shape[0])
        gi = agg @ W_ih.T + b_ih
        gh = node_features @ W_hh.T + b_hh
        i_r, i_z, i_n = jnp.split(gi, 3, axis=1)
        h_r, h_z, h_n = jnp.split(gh, 3, axis=1)
        r = jax.nn.sigmoid(i_r + h_r)
        z = jax.nn.sigmoid(i_z + h_z)
        n = jnp.tanh(i_n + r * h_n)
        return (1.0 - z) * n + z * node_features
    edge_index = jnp.stack([src, dst])
    x = _layernorm(x + _L0_gnn_ref(x, edge_index, L0_gnn_eps, L0_gnn_W1, L0_gnn_b1, L0_gnn_W2, L0_gnn_b2), axis=-1)
    x = _layernorm(x + _L1_gnn_ref(x, edge_index, edge_attr_64, L1_gnn_W1, L1_gnn_b1, L1_gnn_ln_g, L1_gnn_ln_b, L1_gnn_W2, L1_gnn_b2, L1_gnn_gate_w, L1_gnn_gate_b, L1_gnn_W_ih, L1_gnn_b_ih, L1_gnn_W_hh, L1_gnn_b_hh), axis=-1)
    return x

_drawn_inputs = setup_inputs


def setup_inputs(seed=0):
    import zlib

    import numpy as np

    out = dict(_drawn_inputs(seed))
    spreads = {'L0_gnn_b1': (0.0, 0.354),
     'L0_gnn_b2': (0.0, 0.1),
     'L1_gnn_b1': (0.0, 0.1),
     'L1_gnn_ln_g': (1.0, 0.2),
     'L1_gnn_ln_b': (0.0, 0.1),
     'L1_gnn_b2': (0.0, 0.1),
     'L1_gnn_b_ih': (0.0, 0.731),
     'L1_gnn_b_hh': (0.0, 0.8)}
    factors = {}
    for name, (base, spread) in spreads.items():
        noise = np.random.default_rng([zlib.crc32(name.encode()), seed]).standard_normal(out[name].shape)
        drawn = base * np.exp(spread * noise) if base else spread * noise
        out[name] = jnp.asarray(drawn.astype(out[name].dtype))
    for name, factor in factors.items():
        out[name] = (out[name] * factor).astype(out[name].dtype)
    return out
```

```python
import concourse.bass as bass
from concourse import mybir
from contextlib import ExitStack

F32 = mybir.dt.float32
I32 = mybir.dt.int32
ALU = mybir.AluOpType
ACT = mybir.ActivationFunctionType
AX = mybir.AxisListType

P = 128
J = 5
G = P * J
W = 32
U = 4
WIDE = 256
LN_EPS = 1e-5


def bass_gnn_kernel(nc, x, src, dst, edge_attr_64, L0_gnn_eps, L0_gnn_W1, L0_gnn_b1, L0_gnn_W2, L0_gnn_b2,
                    L1_gnn_W1, L1_gnn_b1, L1_gnn_ln_g, L1_gnn_ln_b, L1_gnn_W2, L1_gnn_b2, L1_gnn_gate_w,
                    L1_gnn_gate_b, L1_gnn_W_ih, L1_gnn_b_ih, L1_gnn_W_hh, L1_gnn_b_hh, out):
    N, D = x.shape
    E, ED = edge_attr_64.shape
    T = E // G
    NB = -(-N // P)
    NC = NB // 2
    NW = -(-NB * P // WIDE)
    NPAD = NW * WIDE
    C = ED + W
    M = D + 1
    FR, FG = 125, T // 125
    OFF = 1
    assert D == P and T * G == E and FR * FG == T and NB % 2 == 0

    PD = nc.dram_tensor("P_rows", [NB * P, D], F32, kind="Internal").ap()
    QD = nc.dram_tensor("Q_rows", [NB * P, D], F32, kind="Internal").ap()

    src_v = src.rearrange("(t p j) -> t p j", p=P, j=J)
    dst_v = dst.rearrange("(t p j) -> t p j", p=P, j=J)
    ef_v = edge_attr_64.rearrange("(t p j) d -> t p j d", p=P, j=J)

    with ExitStack() as ctx:
        def sb(name, shape, dt=F32):
            return ctx.enter_context(nc.sbuf_tensor(name, shape, dt))

        def ps(name, shape):
            return ctx.enter_context(nc.psum_tensor(name, shape, F32))

        def sem(name):
            return ctx.enter_context(nc.semaphore(name))

        aggT = sb("aggT", [P, NPAD])
        gsum = sb("gsum", [1, NPAD])
        nodes = sb("nodes", [P, NB, D])
        base_bc = sb("base_bc", [P, T])
        base_i = sb("base_i", [1, T + OFF], I32)
        mean = sb("mean", [P, NB])
        rstd = sb("rstd", [P, NB])
        rtmp = sb("rtmp", [P, NB])
        rvar = sb("rvar", [P, NB])

        idx = sb("idx", [P, U, J], I32)
        idx2 = sb("idx2", [P, J], I32)
        dsti = sb("dsti", [P, U, J], I32)
        drel = sb("drel", [P, U, J])
        rings = sb("rings", [P, U * J * D + U * J * C])
        Gx = rings[:, 0:U * J * D].rearrange("p (u j d) -> p u j d", u=U, j=J)
        Ce = rings[:, U * J * D:].rearrange("p (u j c) -> p u j c", u=U, j=J)
        CTx = sb("CTx", [P, 2 * J * P])
        CT = CTx[0:C, :].rearrange("c (s e) -> c s e", s=2)
        rhs = sb("rhs", [C, U, D + 1])
        h = sb("h", [P, 2, J, D])
        sq = sb("sq", [P, J, D], mybir.dt.bfloat16)
        ss = sb("ss", [P, 2, J])
        lnv = sb("lnv", [P, 2, J])
        r0 = sb("r0", [P, 2, J])
        ra = sb("ra", [P, 2, J])
        rb = sb("rb", [P, 2, J])
        rc = sb("rc", [P, 2, J])
        r1 = sb("r1", [P, 2, J])
        ge = sb("ge", [P, 2, J])
        g1 = sb("g1", [P, 2, J])
        gate = sb("gate", [P, 2, J])
        Sg = sb("Sg", [P, 2, J, W])
        msg = sb("msg", [P, 2, J, M])
        Us = sb("Us", [W, M])

        ident = sb("ident", [P, P])
        ones = sb("ones", [P, P])
        nodes_flat = nodes[:, :, :].rearrange("p b d -> p (b d)")
        iota_i = nodes_flat[:, 12000:12000 + WIDE].bitcast(I32)
        iota = sb("iota", [P, WIDE])
        W1 = sb("W1", [P, D])
        W2 = sb("W2", [P, D])
        b1c = sb("b1c", [P, 1])
        b2bc = sb("b2bc", [P, D])
        eps1 = sb("eps1", [P, 2])
        Wabc = sb("Wabc", [P, 2, D])
        W3g = sb("W3g", [ED, D])
        q_bias = sb("q_bias", [P, 2 * D])
        wmean = sb("wmean", [P, 8])
        g_bc = sb("g_bc", [P, D])
        nb_bc = sb("nb_bc", [P, D])
        lnb_c = sb("lnb_c", [P, 1])
        V2 = sb("V2", [P, D])
        b2row = sb("b2row", [1, 2, D])
        gbias = sb("gbias", [P, 2])
        Wg = nodes_flat[:, 8000:8000 + 6 * D].rearrange("p (a c d) -> p a c d", a=2, c=3)
        WgT = sb("WgT", [P, 2, 3 * D])
        bi = nodes_flat[:, 9000:9000 + 3 * D]
        bh = nodes_flat[:, 10000:10000 + 3 * D]
        b1bc = nodes_flat[:, 6000:6000 + D]
        b_bc = nodes_flat[:, 6200:6200 + D]
        Wab = nodes_flat[:, 6400:6400 + 2 * D].rearrange("p (a d) -> p a d", a=2)
        base_f = nodes_flat[0:1, 7000:7000 + T]
        gb = sb("gb", [P, 4 * D])
        fl = sb("fl", [P, 4])
        fl_i = sb("fl_i", [1, 2], I32)
        epsc = sb("epsc", [P, 1])

        xb = Gx[:, :, 0:2, :]
        yT = h[:, :, 0:2, :]
        hT = msg[:, :, 0:2, 0:D]
        xm = CTx[:, 0:8 * P].rearrange("p (s a n) -> p s a n", s=2, a=2)
        PQ = rings[:, U * J * D:U * J * D + 8 * D].rearrange("p (s a f) -> p s a f", s=2, a=2)
        gin = rings[:, 0:2048].rearrange("p (s a f) -> p s a f", s=2, a=2)
        rz = rings[:, 2048:3072].rearrange("p (s a f) -> p s a f", s=2, a=2)
        wide = rings[:, 2 * J * D:2 * J * D + J * WIDE].rearrange("p (j w) -> p j w", j=J)
        assert J * WIDE <= 2 * J * D
        bn = rings[:, 3100:3100 + NB * 6].rearrange("p (b k) -> p b k", k=6)
        assert 3100 + NB * 6 <= 3712
        x1s = rings[:, 3712:3712 + 4 * D].rearrange("p (s a d) -> p s a d", s=2, a=2)
        h_flat = h[:, :, :, :].rearrange("p s j d -> p (s j d)")
        nn = h_flat[:, 0:4 * D].rearrange("p (s a d) -> p s a d", s=2, a=2)
        dd = h_flat[:, 4 * D:8 * D].rearrange("p (s a d) -> p s a d", s=2, a=2)

        hp = [ps(f"hp{i}", [P, 1024]) for i in range(2)]
        cp = ps("cp", [P, 1024])
        up = ps("up", [P, 512])
        vp = ps("vp", [P, 512])

        s = {}

        def S(name):
            if name not in s:
                s[name] = sem(name)
            return s[name]

        class Step:
            def __init__(self, static, i=None):
                self.static, self.i = static, i

            def back(self, lag):
                return Step(self.static - lag, self.i)

            @property
            def t(self):
                return self.static if self.i is None else self.i * U + self.static

            @property
            def slot(self):
                return self.static % U

            @property
            def lap(self):
                return self.static // U if self.i is None else self.i + self.static // U

            def since(self, first):
                return self.i is not None or self.static >= first

            def within(self, count):
                return self.i is not None or 0 <= self.static < count

        def turns(eng, count, lag, body, top=None, peel=2 * U):
            for k in range(peel):
                body(Step(k), None)
            n = (count - peel) // U
            with eng.Fori(0, n) as i:
                loaded = top(Step(peel, i)) if top else None
                for k in range(U):
                    body(Step(peel + k, i), loaded[k] if loaded else None)
            for k in range(peel + n * U, count + lag):
                body(Step(k), None)

        def settled(eng):
            eng.sem_inc(S("settled"), 1)

        def flag(eng):
            eng.wait_ge(S("flag_ready"), 1)
            return eng.value_load(fl_i[0:1, 0:1], min_val=0, max_val=1)


        def bases(eng, regs, t):
            eng.load(regs, base_i[0:1, bass.ds(t.t + OFF, U)])
            return [eng.snap(r, min_val=0, max_val=N - 1) for r in regs]

        def one_base(eng, t):
            return eng.value_load(base_i[0:1, t.t + OFF:t.t + OFF + 1], min_val=0, max_val=N - 1)

        def blocks(t):
            return bass.ds(t.t * 2, 2)

        def cols(t):
            return bass.ds(t.t * (2 * P), 2 * P)

        def hslots(k):
            return [512 * (j // 3) + (D + 1) * (j % 3) for j in range(J)]

        LAG0, LAG1 = 5, 8
        NPEEL = 4
        HS = hslots(0)
        consts = []

        def row(v):
            return v.rearrange("(a d) -> a d", a=1)

        def col(v):
            return v.rearrange("(d a) -> d a", a=1)

        consts += [
            (W1[:, :], L0_gnn_W1), (W2[:, :], L0_gnn_W2), (b1c[:, :], col(L0_gnn_b1)),
            (b2bc[:, :], row(L0_gnn_b2).to_broadcast([P, D])),
            (eps1[:, 0:1], row(L0_gnn_eps).to_broadcast([P, 1])),
            (Wab[:, 0, :], L1_gnn_W1[0:D, :]), (Wab[:, 1, :], L1_gnn_W1[D:2 * D, :]),
            (W3g[:, :], L1_gnn_W1[2 * D:2 * D + ED, :]),
            (b1bc[:, :], row(L1_gnn_b1).to_broadcast([P, D])),
            (g_bc[:, :], row(L1_gnn_ln_g).to_broadcast([P, D])),
            (b_bc[:, :], row(L1_gnn_ln_b).to_broadcast([P, D])),
            (lnb_c[:, :], col(L1_gnn_ln_b)), (V2[:, :], L1_gnn_W2), (b2row[:, 0, :], row(L1_gnn_b2)),
            (gbias[:, 0:1], row(L1_gnn_gate_b).to_broadcast([P, 1])),
            (Wg[:, 0, :, :], L1_gnn_W_ih.rearrange("(c p) d -> p c d", p=P)),
            (Wg[:, 1, :, :], L1_gnn_W_hh.rearrange("(c p) d -> p c d", p=P)),
            (bi[:, :], row(L1_gnn_b_ih).to_broadcast([P, 3 * D])),
            (bh[:, :], row(L1_gnn_b_hh).to_broadcast([P, 3 * D])),
        ] + [(rhs[0:ED, k, D:D + 1], L1_gnn_gate_w) for k in range(U)]

        block = ctx.enter_context(nc.Block())

        @block.sync
        def _(sp):
            with nc.allow_non_contiguous_dma(reason="small tables"):
                sp.dma_start(aggT[0:FR, 0:FG * G].bitcast(I32),
                             dst.rearrange("(p f) -> p f", p=FR)).then_inc(S("dst_all"), 16)
                sp.dma_start(base_i[0:1, OFF:OFF + T],
                             dst.rearrange("(a t f) -> a t f", a=1, f=G)[:, :, 0]).then_inc(S("base_loaded"), 16)
                for to, frm in consts:
                    sp.dma_start(to, frm).then_inc(S("consts"), 16)
            general = flag(sp)

            def load_group(layer, t):
                if t.since(U):
                    sp.wait_ge(S(f"gathered{layer}_{t.slot}"), t.lap * (16 * J))
                sp.dma_start(idx[:, t.slot, :], src_v[t.t, :, :]).then_inc(S(f"idx{layer}_{t.slot}"), 16)
                if t.since(U):
                    sp.wait_ge(S(f"onehot{layer}"), t.t - (U - 1))
                sp.dma_start(dsti[:, t.slot, :], dst_v[t.t, :, :]).then_inc(S(f"dst{layer}_{t.slot}"), 16)

            with sp.If(general == 0):
                def body(t, base):
                    if t.within(T):
                        load_group(0, t)
                turns(sp, T, 0, body)
            with sp.Else():
                with sp.Fori(0, T) as t:
                    sp.wait_ge(S("g_summed0"), t + 1)
                    sp.dma_start(idx[:, 0, :], src_v[t, :, :]).then_inc(S("g_idx0"), 16)
                    sp.dma_start(dsti[:, 0, :], dst_v[t, :, :]).then_inc(S("g_idx0"), 16)

            sp.wait_ge(S("layer0_summed"), 1)

            def body(t, _):
                if t.since(U):
                    sp.wait_ge(S("z_made"), t.t - (U - 1))
                last = t.i is None and t.static == NC - 1
                for a in range(2):
                    n = min(P, N - (NC - 1) * 2 * P - a * P) if last else P
                    sp.dma_start(xb[0:n, t.slot, a, :],
                                 x[bass.ds(t.t * (2 * P) + a * P, n), :]).then_inc(S(f"x_loaded_{t.slot}"), 16)
            turns(sp, NC, 0, body, peel=NPEEL)

            def body(t, _):
                sp.wait_ge(S("pq_made"), t.t + 1)
                for a, to in enumerate((PD, QD)):
                    sp.dma_start(to[bass.ds(t.t * (2 * P), 2 * P), :].rearrange("(b p) d -> p b d", p=P),
                                 PQ[:, t.slot % 2, :, a * D:(a + 1) * D]).then_inc(S(f"pq_stored_{t.slot % 2}"), 16)
            turns(sp, NC, 0, body, peel=NPEEL)
            sp.wait_ge(S("pq_stored_0"), 32 * (NC - NC // 2))
            sp.wait_ge(S("pq_stored_1"), 32 * (NC // 2))

            with sp.If(general == 0):
                def body(t, base):
                    if not t.within(T):
                        return
                    load_group(1, t)
                    if t.since(U):
                        sp.wait_ge(S("tile_turned"), t.t - (U - 1))
                    sp.dma_start(Ce[:, t.slot, :, 0:ED], ef_v[t.t, :, :, :]).then_inc(S(f"ef_{t.slot}"), 16)
                    if t.since(U):
                        sp.wait_ge(S("h_made"), t.t - (U - 1))
                    if base is None:
                        base = one_base(sp, t)
                    sp.dma_start(rhs[ED:C, t.slot, 0:D], QD[bass.ds(base, W), :]).then_inc(S(f"win_{t.slot}"), 16)
                regs = [sp.alloc_register(f"sp_base{k}") for k in range(U)]
                turns(sp, T, 0, body, top=lambda t: bases(sp, regs, t))
            with sp.Else():
                with sp.Fori(0, T) as t:
                    sp.wait_ge(S("g_summed1"), t + 1)
                    sp.dma_start(idx[:, 0, :], src_v[t, :, :]).then_inc(S("g_idx1"), 16)
                    sp.dma_start(dsti[:, 0, :], dst_v[t, :, :]).then_inc(S("g_idx1"), 16)
                    sp.dma_start(idx2[:, :], dst_v[t, :, :]).then_inc(S("g_idx1"), 16)
                    sp.dma_start(Ce[:, 3, :, 0:ED], ef_v[t, :, :, :]).then_inc(S("g_idx1"), 16)

            def body(t, _):
                sp.wait_ge(S("out_made"), t.t + 1)
                last = t.i is None and t.static == NC - 1
                for a in range(2):
                    n = min(P, N - (NC - 1) * 2 * P - a * P) if last else P
                    sp.dma_start(out[bass.ds(t.t * (2 * P) + a * P, n), :],
                                 xb[0:n, t.slot, a, :]).then_inc(S(f"stored_{t.slot}"), 16)
            turns(sp, NC, 0, body, peel=NPEEL)
            for k in range(U):
                sp.wait_ge(S(f"stored_{k}"), 32 * len(range(k, NC, U)))

        @block.gpsimd
        def _(pool):
            pool.iota(iota_i[:, :], pattern=[[1, WIDE]], base=0, channel_multiplier=0).then_inc(S("iota_made"), 1)
            pool.memset(ones[:, :], 1.0).then_inc(S("ones_made"), 1)
            pool.wait_ge(S("ones_made"), 1)
            pool.affine_select(out=ident[:, :], in_=ones[:, :], compare_op=ALU.is_equal, fill=0.0, base=0,
                               pattern=[[1, P]], channel_multiplier=-1).then_inc(S("ident_made"), 1)
            general = flag(pool)

            def gather(to, table, index, name):
                settled(pool)
                for j in range(J):
                    pool.indirect_dma_start(to[:, j, :], None, table,
                                            bass.IndirectOffsetOnAxis(ap=index[:, j:j + 1], axis=0)).then_inc(S(name), 16)

            for layer, table in ((0, x), (1, PD)):
                if layer:
                    pool.wait_ge(S("pq_stored_0"), 32 * (NC - NC // 2))
                    pool.wait_ge(S("pq_stored_1"), 32 * (NC // 2))
                with pool.If(general == 0):
                    def body(t, _):
                        pool.wait_ge(S(f"idx{layer}_{t.slot}"), (t.lap + 1) * 16)
                        if t.since(U):
                            pool.wait_ge(S("h_added" if layer else "sums_made0"), t.t - (U - 1))
                        gather(Gx[:, t.slot], table, idx[:, t.slot], f"gathered{layer}_{t.slot}")
                    turns(pool, T, 0, body)
                with pool.Else():
                    with pool.Fori(0, T) as t:
                        pool.wait_ge(S(f"g_idx{layer}"), (t + 1) * (64 if layer else 32))
                        gather(Gx[:, 0], table, idx[:, 0], f"g_gathered{layer}")
                        if layer:
                            gather(Gx[:, 1], QD, idx2, f"g_gathered{layer}")

        @block.tensor
        def _(pe):
            pe.wait_ge(S("ident_made"), 1)
            pe.wait_ge(S("range_rows"), 1)
            pe.matmul(up[0:1, 0:FR], fl[0:FR, 2:3], ident[0:FR, 0:FR], start=True, stop=True).then_inc(S("range_row"), 1)
            pe.wait_ge(S("base_float"), 1)
            for a, n in ((0, 512), (512, T - 512)):
                mm = pe.matmul(cp[:, a:a + n], ones[0:1, :], base_f[0:1, a:a + n], start=True, stop=True)
            mm.then_inc(S("base_spread"), 1)
            pe.wait_ge(S("consts"), 16 * len(consts))
            for a in range(2):
                for k in range(3):
                    mm = pe.transpose(hp[a][:, k * P:(k + 1) * P], Wg[:, a, k, :], ident[:, :])
            mm.then_inc(S("gru_turned"), 1)
            pe.matmul(hp[0][0:1, 512:512 + D], lnb_c[:, :], V2[:, :], start=True, stop=True).then_inc(S("b2_made"), 1)
            general = flag(pe)

            def window_sums(layer, t):
                pe.wait_ge(S("msg_made" if layer else "onehot0"), t.t + 1)
                if not layer:
                    pe.wait_ge(S(f"gathered0_{t.slot}"), (t.lap + 1) * (16 * J))
                if t.since(1):
                    pe.wait_ge(S(f"sums_copied{layer}"), t.t)
                for j in range(J):
                    if layer:
                        mm = pe.matmul(up[0:W, 0:M], Sg[:, t.slot % 2, j, :], msg[:, t.slot % 2, j, :],
                                       start=(j == 0), stop=(j == J - 1))
                    else:
                        mm = pe.matmul(up[0:W, 0:D], Ce[:, t.slot, j, ED:C], Gx[:, t.slot, j, :],
                                       start=(j == 0), stop=(j == J - 1))
                mm.then_inc(S(f"sums_made{layer}"), 1)

            def turn_sums(layer, t):
                pe.wait_ge(S(f"sums_copied{layer}"), t.t + 1)
                if t.since(1):
                    pe.wait_ge(S(f"added{layer}"), t.t)
                settled(pe)
                mm = pe.transpose(vp[:, 0:W], Us[:, 0:D], ident[0:W, 0:W])
                if layer:
                    mm = pe.transpose(vp[0:1, W:2 * W], Us[:, D:M], ident[0:W, 0:W])
                mm.then_inc(S(f"sums_turned{layer}"), 1)

            with pe.If(general == 0):
                pe.wait_ge(S("base_saved"), 1)
                def body(t, _):
                    if t.back(2).within(T):
                        window_sums(0, t.back(2))
                    if t.back(3).within(T):
                        turn_sums(0, t.back(3))
                turns(pe, T, LAG0, body)
            with pe.Else():
                with pe.Fori(0, T) as t:
                    with pe.Fori(0, NW) as w:
                        pe.wait_ge(S("g_gathered0"), (t + 1) * (16 * J))
                        pe.wait_ge(S("g_wide0"), t * NW + w + 1)
                        for j in range(J):
                            mm = pe.matmul(cp[:, 0:WIDE], Gx[:, 0, j, :], wide[:, j, :], start=(j == 0), stop=(j == J - 1))
                        mm.then_inc(S("g_sums0"), 1)

            pe.wait_ge(S("layer0_summed"), 1)

            def body(t, _):
                if t.within(NC):
                    pe.wait_ge(S(f"x_loaded_{t.slot}"), (t.lap + 1) * 32)
                    if t.since(2):
                        pe.wait_ge(S("y_made"), t.t - 1)
                    for a in range(2):
                        mm = pe.transpose(cp[:, 512 * (t.slot % 2) + a * P:512 * (t.slot % 2) + (a + 1) * P], xb[:, t.slot, a, :], ident[:, :])
                    mm.then_inc(S("x_turned"), 1)
                b = t.back(1)
                if b.within(NC):
                    pe.wait_ge(S("y_made"), b.t + 1)
                    if b.since(2):
                        pe.wait_ge(S("hidden_made"), b.t - 1)
                    pe.matmul(hp[b.slot % 2][:, 0:2 * P], W1[:, :], yT[:, b.slot % 2], start=True, stop=True).then_inc(S("hidden_mm"), 1)
                c = t.back(2)
                if c.within(NC):
                    pe.wait_ge(S("hidden_made"), c.t + 1)
                    if c.since(2):
                        pe.wait_ge(S("z_made"), c.t - 1)
                    for a in range(2):
                        mm = pe.matmul(hp[c.slot % 2][:, 512 + a * D:512 + (a + 1) * D], hT[:, c.slot % 2, a, :], W2[:, :], start=True, stop=True)
                    mm.then_inc(S("mlp_mm"), 1)
            turns(pe, NC, 3, body, peel=NPEEL)

            def body(t, _):
                if t.within(NC):
                    pe.wait_ge(S("x1_made"), t.t + 1)
                    if t.since(2):
                        pe.wait_ge(S("x1T_copied"), t.t - 1)
                    for a in range(2):
                        mm = pe.transpose(cp[:, 512 * (t.slot % 2) + a * P:512 * (t.slot % 2) + (a + 1) * P],
                                          x1s[:, t.slot % 2, a, :], ident[:, :])
                    mm.then_inc(S("x1_turned"), 1)
                b = t.back(1)
                if b.within(NC):
                    pe.wait_ge(S("x1T_copied"), b.t + 1)
                    if b.since(2):
                        pe.wait_ge(S("pq_made"), b.t - 1)
                    for a in range(2):
                        mm = pe.matmul(hp[b.slot % 2][:, a * 2 * D:(a + 1) * 2 * D], xm[:, b.slot % 2, 0, a * P:(a + 1) * P],
                                       Wabc[:, :, :], start=True, stop=True)
                    mm.then_inc(S("pq_mm"), 1)
            turns(pe, NC, 2, body, peel=NPEEL)

            with pe.If(general == 0):
                def body(t, _):
                    b, c = t.back(1), t.back(2)
                    if b.within(T):
                        pe.wait_ge(S("onehot1"), b.t + 1)
                        pe.wait_ge(S(f"ef_{b.slot}"), (b.lap + 1) * 16)
                        if b.since(1):
                            pe.wait_ge(S("tile_copied"), b.t)
                        for j in range(J):
                            mm = pe.transpose(cp[0:C, j * P:(j + 1) * P], Ce[:, b.slot, j, :], ident[:, :])
                        mm.then_inc(S("tile_turned"), 1)
                    if c.within(T):
                        pe.wait_ge(S("tile_copied"), c.t + 1)
                        pe.wait_ge(S(f"win_{c.slot}"), (c.lap + 1) * 16)
                        if c.since(2):
                            pe.wait_ge(S("h_added"), c.t - 1)
                            pe.wait_ge(S("ge_made"), c.t - 1)
                        for j in range(J):
                            mm = pe.matmul(hp[c.slot % 2][:, HS[j]:HS[j] + D + 1], CT[:, c.slot % 2, j * P:(j + 1) * P],
                                           rhs[:, c.slot, :], start=True, stop=True)
                        mm.then_inc(S("h_made"), 1)
                    if t.back(6).within(T):
                        turn_sums(1, t.back(6))
                    if t.back(5).within(T):
                        window_sums(1, t.back(5))
                turns(pe, T, LAG1, body)
            with pe.Else():
                with pe.Fori(0, T) as t:
                    pe.wait_ge(S("g_idx1"), (t + 1) * 64)
                    settled(pe)
                    for j in range(J):
                        mm = pe.transpose(cp[0:ED, j * P:(j + 1) * P], Ce[:, 3, j, 0:ED], ident[:, :])
                    mm.then_inc(S("g_turned"), 1)
                    pe.wait_ge(S("g_copied"), t + 1)
                    for j in range(J):
                        mm = pe.matmul(hp[0][:, HS[j]:HS[j] + D + 1], CT[0:ED, 0, j * P:(j + 1) * P],
                                       rhs[0:ED, 0, :], start=True, stop=True)
                    mm.then_inc(S("g_h_made"), 1)
                    with pe.Fori(0, NW) as w:
                        pe.wait_ge(S("g_wide1"), t * NW + w + 1)
                        for j in range(J):
                            pe.matmul(cp[:, 0:WIDE], msg[:, 0, j, 0:D], wide[:, j, :], start=(j == 0), stop=(j == J - 1))
                        for j in range(J):
                            mm = pe.matmul(cp[0:1, 512:512 + WIDE], msg[:, 0, j, D:M], wide[:, j, :], start=(j == 0), stop=(j == J - 1))
                        mm.then_inc(S("g_sums1"), 1)

            pe.wait_ge(S("layer1_summed"), 1)

            def body(t, _):
                if t.within(NC):
                    if t.since(2):
                        pe.wait_ge(S("xm_copied"), t.t - 1)
                    pe.wait_ge(S("x1_placed"), t.t + 1)
                    o = 512 * (t.slot % 2)
                    for a in range(2):
                        pe.transpose(cp[:, o + a * P:o + (a + 1) * P], x1s[:, t.slot % 2, a, :], ident[:, :])
                    pe.matmul(cp[:, o + 2 * P:o + 4 * P], V2[:, :], aggT[:, cols(t)], start=True, stop=False)
                    pe.matmul(cp[:, o + 2 * P:o + 4 * P], b2row[0:1, 1, :], gsum[0:1, cols(t)],
                              start=False, stop=True).then_inc(S("xm_mm"), 1)
                b = t.back(1)
                if b.within(NC):
                    pe.wait_ge(S("xm_copied"), b.t + 1)
                    if b.since(2):
                        pe.wait_ge(S("gin_made"), b.t - 1)
                    for a in range(2):
                        to = hp[b.slot % 2][:, 512 * a:512 * (a + 1)]
                        x1T = xm[:, b.slot % 2, 0, a * P:(a + 1) * P]
                        mT = xm[:, b.slot % 2, 1, a * P:(a + 1) * P]
                        pe.matmul(to[:, 0:2 * D], mT, WgT[:, 0, 0:2 * D], start=True, stop=False)
                        pe.matmul(to[:, 0:2 * D], x1T, WgT[:, 1, 0:2 * D], start=False, stop=True)
                        pe.matmul(to[:, 2 * D:3 * D], mT, WgT[:, 0, 2 * D:3 * D], start=True, stop=True)
                        mm = pe.matmul(to[:, 3 * D:4 * D], x1T, WgT[:, 1, 2 * D:3 * D], start=True, stop=True)
                    mm.then_inc(S("gru_mm"), 1)
            turns(pe, NC, 2, body, peel=NPEEL)

        @block.scalar
        def _(act):
            general = flag(act)

            def copy_sums(layer, t):
                act.wait_ge(S(f"sums_made{layer}"), t.t + 1)
                if t.since(1):
                    act.wait_ge(S(f"sums_turned{layer}"), t.t)
                n = M if layer else D
                act.activation(Us[:, 0:n], up[0:W, 0:n], ACT.Copy).then_inc(S(f"sums_copied{layer}"), 1)

            with act.If(general == 0):
                def body(t, _):
                    if t.back(2).within(T):
                        copy_sums(0, t.back(2))
                turns(act, T, LAG0, body)

            act.wait_ge(S("layer0_summed"), 1)

            def body(t, _):
                b = t.back(1)
                if b.within(NC):
                    act.wait_ge(S("hidden_mm"), b.t + 1)
                    if b.since(2):
                        act.wait_ge(S("mlp_mm"), b.t - 1)
                    act.activation(hT[:, b.slot % 2], hp[b.slot % 2][:, 0:2 * P].rearrange("p (a n) -> p a n", a=2), ACT.Relu,
                                   bias=b1c[:, 0:1]).then_inc(S("hidden_made"), 1)
            turns(act, NC, 3, body, peel=NPEEL)

            def std(n):
                act.wait_ge(S("var_made"), n)
                act.activation(rtmp[:, :], rvar[:, :], ACT.Sqrt).then_inc(S("std_made"), 1)
            std(1)

            def body(t, _):
                if t.within(NC):
                    act.wait_ge(S("x1_made"), t.t + 1)
                    act.activation(nodes[:, blocks(t), :], x1s[:, t.slot % 2], ACT.Copy).then_inc(S("x1_kept"), 1)
                    act.wait_ge(S("x1_turned"), t.t + 1)
                    if t.since(2):
                        act.wait_ge(S("pq_mm"), t.t - 1)
                    act.activation(xm[:, t.slot % 2, 0, :], cp[:, 512 * (t.slot % 2):512 * (t.slot % 2) + 2 * P],
                                   ACT.Copy).then_inc(S("x1T_copied"), 1)
            turns(act, NC, 2, body, peel=NPEEL)

            def gate_exp(k, name):
                for lo, hi in ((0, 3), (3, J)):
                    a = act.activation(ge[:, k, lo:hi].unsqueeze(2),
                                       hp[k][:, HS[lo]:HS[lo] + (hi - lo) * (D + 1)].rearrange("p (j f) -> p j f", f=D + 1)[:, :, D:D + 1],
                                       ACT.Exp, scale=-1.0, bias=gbias[:, 1:2])
                a.then_inc(S(name), 1)

            def guess(k, sums, logs, name, n):
                for j in range(J):
                    a = act.activation(sq[:, j, :], h[:, k, j, :], ACT.Square, accum_out=ss[:, k, j:j + 1])
                a.then_inc(S(sums), 1)
                act.wait_ge(S(sums), n)
                act.activation(lnv[:, k, :], ss[:, k, :], ACT.Ln, scale=1.0 / D, bias=epsc[:, 0:1]).then_inc(S(logs), 1)
                act.wait_ge(S(logs), n)
                act.activation(r0[:, k, :], lnv[:, k, :], ACT.Exp, scale=-0.5).then_inc(S(name), 1)

            act.preload_act_table_set("natural_log_exp_and_others")
            with act.If(general == 0):
                def body(t, _):
                    b, c = t.back(1), t.back(3)
                    if c.within(T):
                        act.wait_ge(S("h_made"), c.t + 1)
                        if c.since(2):
                            act.wait_ge(S("msg_made"), c.t - 1)
                        gate_exp(c.slot % 2, "ge_made")
                    if t.back(6).within(T):
                        copy_sums(1, t.back(6))
                    if b.within(T):
                        act.wait_ge(S("tile_turned"), b.t + 1)
                        if b.since(2):
                            act.wait_ge(S("h_made"), b.t - 1)
                        act.activation(CT[:, b.slot % 2, :], cp[0:C, 0:J * P], ACT.Copy).then_inc(S("tile_copied"), 1)
                    if c.within(T):
                        act.wait_ge(S("h_added"), c.t + 1)
                        if c.since(1):
                            act.wait_ge(S("squares"), c.t)
                        guess(c.slot % 2, "squares", "logs", "r0_made", c.t + 1)
                turns(act, T, LAG1, body)
            with act.Else():
                with act.Fori(0, T) as t:
                    act.wait_ge(S("g_turned"), t + 1)
                    act.activation(CT[0:ED, 0, :], cp[0:ED, 0:J * P], ACT.Copy).then_inc(S("g_copied"), 1)
                    act.wait_ge(S("g_h_made"), t + 1)
                    gate_exp(0, "g_ge_made")
                    act.wait_ge(S("g_h_added"), t + 1)
                    guess(0, "g_squares", "g_logs", "g_r0_made", t + 1)

            act.wait_ge(S("layer1_summed"), 1)

            def body(t, _):
                if t.within(NC):
                    k = t.slot % 2
                    if t.since(2):
                        act.wait_ge(S("xm_mm"), t.t - 1)
                    act.activation(x1s[:, k], nodes[:, blocks(t), :], ACT.Copy).then_inc(S("x1_placed"), 1)
                    act.wait_ge(S("xm_mm"), t.t + 1)
                    if t.since(2):
                        act.wait_ge(S("gru_mm"), t.t - 1)
                    act.activation(xm[:, k], cp[:, 512 * k:512 * (k + 1)].rearrange("p (a n) -> p a n", a=2), ACT.Copy).then_inc(S("xm_copied"), 1)
                b = t.back(2)
                if b.within(NC):
                    k = b.slot % 2
                    act.wait_ge(S("gin_made"), b.t + 1)
                    if b.since(2):
                        act.wait_ge(S("z2_made"), b.t - 1)
                    act.activation(rz[:, k], gin[:, k, :, 0:2 * D], ACT.Sigmoid).then_inc(S("rz_made"), 1)
                c = t.back(3)
                if c.within(NC):
                    k = c.slot % 2
                    act.wait_ge(S("n_in"), c.t + 1)
                    act.activation(nn[:, k], nn[:, k], ACT.Tanh).then_inc(S("n_made"), 1)
            turns(act, NC, 4, body, peel=NPEEL)
            std(2)

        @block.vector
        def _(v):
            v.wait_ge(S("dst_all"), 16)
            allv = aggT[0:FR, 0:FG * G].bitcast(I32).rearrange("p (g f) -> p g f", f=G)
            relv = nodes[:, :, :].rearrange("p b d -> p (b d)")[0:FR, 0:FG * G].rearrange("p (g f) -> p g f", f=G)
            v.tensor_tensor(relv, allv, allv[:, :, 0:1].to_broadcast([FR, FG, G]), ALU.subtract).then_inc(S("rel"), 1)
            v.wait_ge(S("rel"), 1)
            v.tensor_reduce(fl[0:FR, 0:1], relv, AX.XY, ALU.max)
            v.tensor_reduce(fl[0:FR, 1:2], relv, AX.XY, ALU.min).then_inc(S("rel"), 1)
            v.wait_ge(S("rel"), 2)
            v.tensor_scalar(fl[0:FR, 3:4], fl[0:FR, 0:1], float(-(W - 1)), None, ALU.add).then_inc(S("rel"), 1)
            v.wait_ge(S("rel"), 3)
            v.scalar_tensor_tensor(fl[0:FR, 2:3], fl[0:FR, 1:2], -1.0, fl[0:FR, 3:4], ALU.mult, ALU.max).then_inc(S("range_rows"), 1)
            v.wait_ge(S("base_loaded"), 16)
            v.tensor_copy(base_f[:, :], base_i[0:1, OFF:OFF + T]).then_inc(S("base_float"), 1)
            v.wait_ge(S("range_row"), 1)
            v.tensor_reduce(rtmp[0:1, 0:1], up[0:1, 0:FR], AX.X, ALU.max).then_inc(S("rel"), 1)
            v.wait_ge(S("rel"), 4)
            v.tensor_scalar(fl_i[0:1, 0:1], rtmp[0:1, 0:1], 0.0, None, ALU.is_gt).then_inc(S("flag_ready"), 1)
            v.wait_ge(S("base_spread"), 1)
            v.tensor_copy(base_bc[:, :], cp[:, 0:T])
            v.wait_ge(S("iota_made"), 1)
            v.tensor_copy(iota[:, :], iota_i[:, :])
            v.memset(aggT[:, :], 0.0)
            v.memset(gsum[:, :], 0.0).then_inc(S("base_saved"), 1)
            v.wait_ge(S("base_saved"), 1)
            general = flag(v)

            def onehot(layer, t):
                v.wait_ge(S(f"dst{layer}_{t.slot}"), (t.lap + 1) * 16)
                if t.since(1):
                    v.wait_ge(S(f"onehot{layer}"), t.t)
                v.tensor_scalar(drel[:, t.slot, :], dsti[:, t.slot, :], base_bc[:, t.t:t.t + 1] if t.i is None else base_bc[:, bass.ds(t.t, 1)],
                                None, ALU.subtract).then_inc(S(f"drel{layer}"), 1)
                if layer:
                    yield
                v.wait_ge(S(f"drel{layer}"), t.t + 1)
                if t.since(U):
                    v.wait_ge(S("tile_turned" if layer else "sums_made0"), t.t - (U - 1))
                if layer and t.since(U):
                    v.wait_ge(S("Sg_made"), t.t - (U - 1))
                v.tensor_tensor(Ce[:, t.slot, :, ED:C], iota[:, None, 0:W].to_broadcast([P, J, W]),
                                drel[:, t.slot, :, None].to_broadcast([P, J, W]), ALU.is_equal).then_inc(S(f"onehot{layer}"), 1)

            def add(layer, t, base):
                if base is None:
                    base = one_base(v, t)
                v.wait_ge(S(f"sums_turned{layer}"), t.t + 1)
                if t.since(1):
                    v.wait_ge(S(f"added{layer}"), t.t)
                a = v.tensor_tensor(aggT[:, bass.ds(base, W)], aggT[:, bass.ds(base, W)], vp[:, 0:W], ALU.add)
                if layer:
                    a = v.tensor_tensor(gsum[0:1, bass.ds(base, W)], gsum[0:1, bass.ds(base, W)], vp[0:1, W:2 * W], ALU.add)
                a.then_inc(S(f"added{layer}"), 1)

            def add_wide(layer, t):
                v.tensor_copy(drel[:, 0, :], dsti[:, 0, :]).then_inc(S(f"g_drel{layer}"), 1)
                with v.Fori(0, NW) as w:
                    v.wait_ge(S(f"g_drel{layer}"), t * (NW + 1) + w + 1)
                    for j in range(J):
                        if layer:
                            a = v.tensor_scalar(wide[:, j, :], iota[:, :], drel[:, 0, j:j + 1], gate[:, 0, j:j + 1], ALU.is_equal, ALU.mult)
                        else:
                            a = v.tensor_scalar(wide[:, j, :], iota[:, :], drel[:, 0, j:j + 1], None, ALU.is_equal)
                    a.then_inc(S(f"g_wide{layer}"), 1)
                    v.wait_ge(S(f"g_wide{layer}"), t * NW + w + 1)
                    v.tensor_scalar(drel[:, 0, :], drel[:, 0, :], float(-WIDE), None, ALU.add).then_inc(S(f"g_drel{layer}"), 1)
                    v.wait_ge(S(f"g_sums{layer}"), t * NW + w + 1)
                    to = bass.ds(w * WIDE, WIDE)
                    a = v.tensor_tensor(aggT[:, to], aggT[:, to], cp[:, 0:WIDE], ALU.add)
                    if layer:
                        a = v.tensor_tensor(gsum[0:1, to], gsum[0:1, to], cp[0:1, 512:512 + WIDE], ALU.add)
                    a.then_inc(S(f"g_added{layer}"), 1)
                v.wait_ge(S(f"g_added{layer}"), t * NW + NW)
                v.memset(fl[:, 0:1], 0.0).then_inc(S(f"g_summed{layer}"), 1)

            regs = [v.alloc_register(f"dve_base{k}") for k in range(U)]
            with v.If(general == 0):
                def body(t, base):
                    if t.back(3).within(T):
                        add(0, t.back(3), base)
                    if t.within(T):
                        for _ in onehot(0, t):
                            pass
                turns(v, T, LAG0, body, top=lambda t: bases(v, regs, t.back(3)))
                v.wait_ge(S("added0"), T)
            with v.Else():
                v.memset(fl[:, 0:1], 0.0).then_inc(S("g_summed0"), 1)
                with v.Fori(0, T) as t:
                    v.wait_ge(S("g_idx0"), (t + 1) * 32)
                    v.wait_ge(S("g_summed0"), t + 1)
                    add_wide(0, t)
            v.memset(fl[:, 0:1], 0.0).then_inc(S("layer0_summed"), 1)
            v.wait_ge(S("layer0_summed"), 1)

            v.wait_ge(S("consts"), 16 * len(consts))
            steps = [0]

            def step(ins):
                steps[0] += 1
                ins.then_inc(S("tables"), 1)

            def after():
                v.wait_ge(S("tables"), steps[0])
            v.tensor_scalar(eps1[:, 1:2], eps1[:, 0:1], 1.0, None, ALU.add)
            v.memset(epsc[:, :], LN_EPS)
            v.memset(msg[:, :, :, D:M], 1.0)
            v.memset(q_bias[:, 0:D], 0.0)
            for k in range(U):
                v.memset(rhs[ED:C, k, D:D + 1], 0.0)
            v.tensor_scalar(gbias[:, 1:2], gbias[:, 0:1], -1.0, None, ALU.mult)
            v.tensor_scalar(nb_bc[:, :], b_bc[:, :], -1.0, None, ALU.mult)
            v.tensor_tensor(gb[:, 0:2 * D], bi[:, 0:2 * D], bh[:, 0:2 * D], ALU.add)
            v.tensor_copy(gb[:, 2 * D:3 * D], bi[:, 2 * D:3 * D])
            v.tensor_copy(gb[:, 3 * D:4 * D], bh[:, 2 * D:3 * D])
            v.wait_ge(S("gru_turned"), 1)
            for a in range(2):
                v.tensor_copy(WgT[:, a, :], hp[a][:, 0:3 * D])
            v.wait_ge(S("b2_made"), 1)
            v.tensor_tensor(b2row[0:1, 1, :], b2row[0:1, 0, :], hp[0][0:1, 512:512 + D], ALU.add)
            v.tensor_reduce(wmean[:, 0:2], Wab[:, :, :], AX.X, ALU.add)
            v.tensor_reduce(wmean[0:ED, 2:3], W3g[:, :], AX.X, ALU.add)
            step(v.tensor_reduce(wmean[:, 3:4], b1bc[:, :], AX.X, ALU.add))
            after()
            step(v.tensor_scalar(wmean[:, 4:6], wmean[:, 0:2], -1.0 / D, None, ALU.mult))
            step(v.tensor_scalar(wmean[0:ED, 6:7], wmean[0:ED, 2:3], -1.0 / D, None, ALU.mult))
            step(v.tensor_scalar(wmean[:, 7:8], wmean[:, 3:4], -1.0 / D, None, ALU.mult))
            after()
            for a in range(2):
                v.tensor_scalar(Wabc[:, a, :], Wab[:, a, :], wmean[:, 4 + a:5 + a], None, ALU.add)
            for k in range(U):
                v.tensor_scalar(rhs[0:ED, k, 0:D], W3g[:, :], wmean[0:ED, 6:7], None, ALU.add)
            step(v.tensor_scalar(q_bias[:, D:2 * D], b1bc[:, :], wmean[:, 7:8], None, ALU.add))
            after()

            def rows_stats(t, made):
                v.wait_ge(S(made), t.t + 1)
                settled(v)
                for a in range(2):
                    b = v.bn_stats(bn[:, bass.ds(t.t * 2 + a, 1), :], nodes[:, bass.ds(t.t * 2 + a, 1), :])
                b.then_inc(S(made + "_stats"), 1)

            def all_rstd(n, made):
                v.wait_ge(S(made + "_stats"), NC)
                v.tensor_tensor(mean[:, :], bn[:, :, 1], bn[:, :, 4], ALU.add)
                v.tensor_tensor(rtmp[:, :], bn[:, :, 1], bn[:, :, 4], ALU.subtract)
                step(v.tensor_tensor(rvar[:, :], bn[:, :, 2], bn[:, :, 5], ALU.add))
                after()
                v.tensor_scalar(mean[:, :], mean[:, :], 0.5, None, ALU.mult)
                v.scalar_tensor_tensor(rstd[:, :], rtmp[:, :], 0.25, rtmp[:, :], ALU.mult, ALU.mult)
                step(v.tensor_scalar(rvar[:, :], rvar[:, :], 1.0 / D, LN_EPS, ALU.mult, ALU.add))
                after()
                v.tensor_tensor(rvar[:, :], rvar[:, :], rstd[:, :], ALU.add).then_inc(S("var_made"), 1)
                v.wait_ge(S("std_made"), n)
                step(v.reciprocal(rstd[:, :], rtmp[:, :]))
                after()
                step(v.tensor_tensor(rtmp[:, :], rstd[:, :], rstd[:, :], ALU.mult))
                after()
                step(v.scalar_tensor_tensor(rtmp[:, :], rtmp[:, :], -0.5, rvar[:, :], ALU.mult, ALU.mult))
                after()
                step(v.scalar_tensor_tensor(rstd[:, :], rtmp[:, :], 1.5, rstd[:, :], ALU.add, ALU.mult))
                after()

            def body(t, _):
                k = t.slot % 2
                if t.within(NC):
                    v.wait_ge(S("x_turned"), t.t + 1)
                    if t.since(2):
                        v.wait_ge(S("hidden_mm"), t.t - 1)
                    v.scalar_tensor_tensor(yT[:, k].rearrange("p a n -> p (a n)"), cp[:, 512 * k:512 * k + 2 * P], eps1[:, 1:2],
                                           aggT[:, cols(t)], ALU.mult, ALU.add).then_inc(S("y_made"), 1)
                c = t.back(2)
                if c.within(NC):
                    v.wait_ge(S("mlp_mm"), c.t + 1)
                    v.tensor_tensor(nodes[:, blocks(c), :], hp[c.slot % 2][:, 512:512 + 2 * D].rearrange("p (a d) -> p a d", a=2),
                                    xb[:, c.slot, :, :], ALU.add).then_inc(S("z_made"), 1)
                    v.wait_ge(S("z_made"), c.t + 1)
                    v.tensor_tensor(nodes[:, blocks(c), :], nodes[:, blocks(c), :],
                                    b2bc[:, None, :].to_broadcast([P, 2, D]), ALU.add).then_inc(S("z"), 1)
                    rows_stats(c, "z")
            turns(v, NC, 3, body, peel=NPEEL)
            all_rstd(1, "z")

            def body(t, _):
                if t.within(NC):
                    if t.since(2):
                        v.wait_ge(S("x1_turned"), t.t - 1)
                        v.wait_ge(S("x1_kept"), t.t - 1)
                    for a in range(2):
                        b = bass.ds(t.t * 2 + a, 1)
                        o = v.tensor_scalar(x1s[:, t.slot % 2, a:a + 1, :], nodes[:, b, :], mean[:, b], rstd[:, b], ALU.subtract, ALU.mult)
                    o.then_inc(S("x1_made"), 1)
                b = t.back(1)
                if b.within(NC):
                    k = b.slot % 2
                    v.wait_ge(S("pq_mm"), b.t + 1)
                    if b.since(2):
                        v.wait_ge(S(f"pq_stored_{k}"), (b.lap * 2 + (b.slot // 2)) * 32)
                    v.tensor_tensor(PQ[:, k], hp[k][:, 0:4 * D].rearrange("p (a f) -> p a f", a=2),
                                    q_bias[:, None, :].to_broadcast([P, 2, 2 * D]), ALU.add).then_inc(S("pq_made"), 1)
            turns(v, NC, 2, body, peel=NPEEL)

            v.memset(aggT[:, :], 0.0).then_inc(S("sums_cleared"), 1)
            v.wait_ge(S("sums_cleared"), 1)

            def newton_a(k, name):
                v.tensor_tensor(ra[:, k, :], r0[:, k, :], r0[:, k, :], ALU.mult)
                v.tensor_scalar(rb[:, k, :], ss[:, k, :], -0.5 / D, -0.5 * LN_EPS, ALU.mult, ALU.add)
                v.tensor_scalar(g1[:, k, :], ge[:, k, :], 1.0, None, ALU.add).then_inc(S(name), 1)

            def newton_b(k, name):
                v.tensor_tensor(rc[:, k, :], ra[:, k, :], rb[:, k, :], ALU.mult)
                v.reciprocal(gate[:, k, :], g1[:, k, :]).then_inc(S(name), 1)

            def newton_c(k, name):
                v.scalar_tensor_tensor(r1[:, k, :], rc[:, k, :], 1.5, r0[:, k, :], ALU.add, ALU.mult).then_inc(S(name), 1)

            def scaled(k, name):
                for j in range(J):
                    a = v.scalar_tensor_tensor(msg[:, k, j, 0:D], h[:, k, j, :], r1[:, k, j:j + 1], g_bc[:, :], ALU.mult, ALU.mult)
                a.then_inc(S(name), 1)

            def clipped(k, name):
                v.tensor_tensor(msg[:, k, :, 0:D], msg[:, k, :, 0:D], nb_bc[:, None, :].to_broadcast([P, J, D]), ALU.max).then_inc(S(name), 1)

            def add_rows(to, k, rows, part):
                lo, hi = ((0, 3), (3, J))[part]
                return v.tensor_tensor(h[:, k, lo:hi, :],
                                       to[:, HS[lo]:HS[lo] + (hi - lo) * (D + 1)].rearrange("p (j f) -> p j f", f=D + 1)[:, :, 0:D],
                                       rows[:, lo:hi, :], ALU.add)

            with v.If(general == 0):
                def body(t, base):
                    d, c, e = t.back(4), t.back(3), t.back(7)
                    first = onehot(1, t) if t.within(T) else iter(())
                    next(first, None)
                    if d.within(T):
                        k = d.slot % 2
                        v.wait_ge(S("r0_made"), d.t + 1)
                        newton_a(k, "newton_a")
                    if c.within(T):
                        v.wait_ge(S("h_made"), c.t + 1)
                        v.wait_ge(S("ge_made"), c.t + 1)
                        v.wait_ge(S(f"gathered1_{c.slot}"), (c.lap + 1) * (16 * J))
                        if c.since(2):
                            v.wait_ge(S("scaled"), c.t - 1)
                        add_rows(hp[c.slot % 2], c.slot % 2, Gx[:, c.slot], 0)
                    if d.within(T):
                        v.wait_ge(S("newton_a"), d.t + 1)
                        newton_b(k, "newton_b")
                    if c.within(T):
                        add_rows(hp[c.slot % 2], c.slot % 2, Gx[:, c.slot], 1).then_inc(S("h_added"), 1)
                    if d.within(T):
                        v.wait_ge(S("newton_b"), d.t + 1)
                        newton_c(k, "newton_c")
                        if d.since(2):
                            v.wait_ge(S("sums_made1"), d.t - 1)
                        v.tensor_tensor(Sg[:, k], Ce[:, d.slot, :, ED:C], gate[:, k, :, None].to_broadcast([P, J, W]),
                                        ALU.mult).then_inc(S("Sg_made"), 1)
                    for _ in first:
                        pass
                    if d.within(T):
                        v.wait_ge(S("newton_c"), d.t + 1)
                        scaled(k, "scaled")
                    if e.within(T):
                        add(1, e, base)
                    if d.within(T):
                        v.wait_ge(S("scaled"), d.t + 1)
                        clipped(k, "msg_made")
                turns(v, T, LAG1, body, top=lambda t: bases(v, regs, t.back(7)))
                v.wait_ge(S("added1"), T)
            with v.Else():
                v.memset(fl[:, 0:1], 0.0).then_inc(S("g_summed1"), 1)
                with v.Fori(0, T) as t:
                    v.wait_ge(S("g_h_made"), t + 1)
                    v.wait_ge(S("g_ge_made"), t + 1)
                    v.wait_ge(S("g_gathered1"), (t + 1) * (32 * J))
                    v.wait_ge(S("g_summed1"), t + 1)
                    add_rows(hp[0], 0, Gx[:, 0], 0)
                    add_rows(hp[0], 0, Gx[:, 0], 1).then_inc(S("g_rows"), 1)
                    v.wait_ge(S("g_rows"), t + 1)
                    v.tensor_tensor(h[:, 0], h[:, 0], Gx[:, 1], ALU.add).then_inc(S("g_h_added"), 1)
                    v.wait_ge(S("g_r0_made"), t + 1)
                    newton_a(0, "g_newton_a")
                    v.wait_ge(S("g_newton_a"), t + 1)
                    newton_b(0, "g_newton_b")
                    v.wait_ge(S("g_newton_b"), t + 1)
                    newton_c(0, "g_newton_c")
                    v.wait_ge(S("g_newton_c"), t + 1)
                    scaled(0, "g_scaled")
                    v.wait_ge(S("g_scaled"), t + 1)
                    clipped(0, "g_msg_made")
                    v.wait_ge(S("g_msg_made"), t + 1)
                    add_wide(1, t)
            v.memset(fl[:, 0:1], 0.0).then_inc(S("layer1_summed"), 1)
            v.wait_ge(S("layer1_summed"), 1)

            def body(t, _):
                b = t.back(1)
                if b.within(NC):
                    k = b.slot % 2
                    v.wait_ge(S("gru_mm"), b.t + 1)
                    if b.since(2):
                        v.wait_ge(S("rz_made"), b.t - 1)
                        v.wait_ge(S("n_in"), b.t - 1)
                    v.tensor_tensor(gin[:, k], hp[k][:, :].rearrange("p (a f) -> p a f", a=2),
                                    gb[:, None, :].to_broadcast([P, 2, 4 * D]), ALU.add).then_inc(S("gin_made"), 1)
                c = t.back(2)
                if c.within(NC):
                    k = c.slot % 2
                    v.wait_ge(S("rz_made"), c.t + 1)
                    if c.since(2):
                        v.wait_ge(S("z2_made"), c.t - 1)
                    v.tensor_tensor(nn[:, k], rz[:, k, :, 0:D], gin[:, k, :, 3 * D:4 * D], ALU.mult).then_inc(S("rh"), 1)
                d = t.back(3)
                if d.within(NC):
                    kd = d.slot % 2
                    v.wait_ge(S("n_made"), d.t + 1)
                    v.tensor_tensor(dd[:, kd], nodes[:, blocks(d), :], nn[:, kd], ALU.subtract).then_inc(S("d1"), 1)
                if c.within(NC):
                    v.wait_ge(S("rh"), c.t + 1)
                    v.tensor_tensor(nn[:, k], nn[:, k], gin[:, k, :, 2 * D:3 * D], ALU.add).then_inc(S("n_in"), 1)
                if d.within(NC):
                    v.wait_ge(S("d1"), d.t + 1)
                    v.tensor_tensor(dd[:, kd], dd[:, kd], rz[:, kd, :, D:2 * D], ALU.mult).then_inc(S("d2"), 1)
                    v.tensor_tensor(nn[:, kd], nn[:, kd], nodes[:, blocks(d), :], ALU.add).then_inc(S("d3"), 1)
                    v.wait_ge(S("d3"), d.t + 1)
                    v.tensor_tensor(nodes[:, blocks(d), :], nn[:, kd], dd[:, kd], ALU.add).then_inc(S("z2_made"), 1)
                    rows_stats(d, "z2_made")
            turns(v, NC, 4, body, peel=NPEEL)
            all_rstd(2, "z2_made")

            def body(t, _):
                if t.since(U):
                    v.wait_ge(S(f"stored_{t.slot}"), t.lap * 32)
                for a in range(2):
                    b = bass.ds(t.t * 2 + a, 1)
                    o = v.tensor_scalar(xb[:, t.slot, a:a + 1, :], nodes[:, b, :], mean[:, b], rstd[:, b], ALU.subtract, ALU.mult)
                o.then_inc(S("out_made"), 1)
            turns(v, NC, 0, body, peel=NPEEL)


_INS = ['x', 'src', 'dst', 'edge_attr_64', 'L0_gnn_eps', 'L0_gnn_W1', 'L0_gnn_b1', 'L0_gnn_W2', 'L0_gnn_b2',
        'L1_gnn_W1', 'L1_gnn_b1', 'L1_gnn_ln_g', 'L1_gnn_ln_b', 'L1_gnn_W2', 'L1_gnn_b2', 'L1_gnn_gate_w',
        'L1_gnn_gate_b', 'L1_gnn_W_ih', 'L1_gnn_b_ih', 'L1_gnn_W_hh', 'L1_gnn_b_hh']


def kernel(**inputs):
    import numpy as _np
    import concourse.bacc as _bacc
    from concourse import mybir as _mybir
    from concourse.bass_utils import run_bass_kernel_spmd as _run

    nc = _bacc.Bacc("TRN2", target_bir_lowering=False, num_devices=1)
    arrays, args = {}, []
    for name in _INS:
        a = _np.ascontiguousarray(inputs[name])
        arrays[f"in_{name}_dram"] = a
        args.append(nc.dram_tensor(f"in_{name}_dram", a.shape, _mybir.dt.from_np(a.dtype), kind="ExternalInput").ap())
    o = nc.dram_tensor("out_0_dram", inputs['x'].shape, _mybir.dt.float32, kind="ExternalOutput").ap()
    bass_gnn_kernel(nc, *args, o)
    r = _run(nc, [arrays], core_ids=[0])
    return r.results[0]["out_0_dram"]
```

```python
import concourse.bass as bass
from concourse import mybir
from contextlib import ExitStack

F32 = mybir.dt.float32
I32 = mybir.dt.int32
ALU = mybir.AluOpType
ACT = mybir.ActivationFunctionType
AX = mybir.AxisListType

P = 128
J = 5
G = P * J
W = 32
U = 4
WIDE = 256
LN_EPS = 1e-5


def bass_gnn_kernel(nc, x, src, dst, edge_attr_64, L0_gnn_eps, L0_gnn_W1, L0_gnn_b1, L0_gnn_W2, L0_gnn_b2,
                    L1_gnn_W1, L1_gnn_b1, L1_gnn_ln_g, L1_gnn_ln_b, L1_gnn_W2, L1_gnn_b2, L1_gnn_gate_w,
                    L1_gnn_gate_b, L1_gnn_W_ih, L1_gnn_b_ih, L1_gnn_W_hh, L1_gnn_b_hh, out):
    N, D = x.shape
    E, ED = edge_attr_64.shape
    T = E // G
    NB = -(-N // P)
    NC = NB // 2
    R = N * U // T
    NT = -(-N // R)
    NW = -(-NB * P // WIDE)
    NPAD = NW * WIDE
    C = ED + W
    M = D + 1
    FR, FG = 125, T // 125
    OFF = 1
    SLACK = 5
    assert D == P and T * G == E and FR * FG == T and NB % 2 == 0 and R * T == N * U and R <= P

    X1D = nc.dram_tensor("x1_rows", [NT * R, D], F32, kind="Internal").ap()
    PD = nc.dram_tensor("P_rows", [NT * R, D], F32, kind="Internal").ap()
    QD = nc.dram_tensor("Q_rows", [NT * R, D], F32, kind="Internal").ap()

    src_v = src.rearrange("(t p j) -> t p j", p=P, j=J)
    dst_v = dst.rearrange("(t p j) -> t p j", p=P, j=J)
    ef_v = edge_attr_64.rearrange("(t p j) d -> t p j d", p=P, j=J)

    with ExitStack() as ctx:
        def sb(name, shape, dt=F32):
            return ctx.enter_context(nc.sbuf_tensor(name, shape, dt))

        def ps(name, shape):
            return ctx.enter_context(nc.psum_tensor(name, shape, F32))

        def sem(name):
            return ctx.enter_context(nc.semaphore(name))

        aggT = sb("aggT", [P, max(NPAD, NT * R)])
        gsum = sb("gsum", [1, NPAD])
        nodes = sb("nodes", [P, NB, D])
        base_bc = sb("base_bc", [P, T])
        base_i = sb("base_i", [1, T + OFF], I32)
        mean = sb("mean", [P, NB])
        rstd = sb("rstd", [P, NB])
        rtmp = sb("rtmp", [P, NB])
        rvar = sb("rvar", [P, NB])

        idx = sb("idx", [P, U, J], I32)
        idx2 = sb("idx2", [P, J], I32)
        dsti = sb("dsti", [P, U, J], I32)
        drel = sb("drel", [P, U, J])
        rings = sb("rings", [P, U * J * D + U * J * C])
        Gx = rings[:, 0:U * J * D].rearrange("p (u j d) -> p u j d", u=U, j=J)
        Ce = rings[:, U * J * D:].rearrange("p (u j c) -> p u j c", u=U, j=J)
        CTx = sb("CTx", [P, 2 * J * P])
        CT = CTx[0:C, :].rearrange("c (s e) -> c s e", s=2)
        rhs = sb("rhs", [C, U, D + 1])
        h = sb("h", [P, 2, J, D])
        sq = sb("sq", [P, J, D], mybir.dt.bfloat16)
        ss = sb("ss", [P, 2, J])
        lnv = sb("lnv", [P, 2, J])
        r0 = sb("r0", [P, 2, J])
        ra = sb("ra", [P, 2, J])
        rb = sb("rb", [P, 2, J])
        rc = sb("rc", [P, 2, J])
        r1 = sb("r1", [P, 2, J])
        ge = sb("ge", [P, 2, J])
        g1 = sb("g1", [P, 2, J])
        gate = sb("gate", [P, 2, J])
        Sg = sb("Sg", [P, 2, J, W])
        msg = sb("msg", [P, 2, J, M])
        Us = sb("Us", [W, M])

        ident = sb("ident", [P, P])
        ones = sb("ones", [P, P])
        nodes_flat = nodes[:, :, :].rearrange("p b d -> p (b d)")
        iota_i = nodes_flat[:, 12000:12000 + WIDE].bitcast(I32)
        iota = sb("iota", [P, WIDE])
        W1 = sb("W1", [P, D])
        W2 = sb("W2", [P, D])
        b1c = sb("b1c", [P, 1])
        b2bc = sb("b2bc", [P, D])
        eps1 = sb("eps1", [P, 2])
        Wabc = sb("Wabc", [P, 2, D])
        W3g = sb("W3g", [ED, D])
        q_bias = sb("q_bias", [P, 2 * D])
        wmean = sb("wmean", [P, 8])
        g_bc = sb("g_bc", [P, D])
        nb_bc = sb("nb_bc", [P, D])
        lnb_c = sb("lnb_c", [P, 1])
        V2 = sb("V2", [P, D])
        b2row = sb("b2row", [1, 2, D])
        gbias = sb("gbias", [P, 2])
        Wg = nodes_flat[:, 8000:8000 + 6 * D].rearrange("p (a c d) -> p a c d", a=2, c=3)
        WgT = sb("WgT", [P, 2, 3 * D])
        bi = nodes_flat[:, 9000:9000 + 3 * D]
        bh = nodes_flat[:, 10000:10000 + 3 * D]
        b1bc = nodes_flat[:, 6000:6000 + D]
        b_bc = nodes_flat[:, 6200:6200 + D]
        Wab = nodes_flat[:, 6400:6400 + 2 * D].rearrange("p (a d) -> p a d", a=2)
        base_f = nodes_flat[0:1, 7000:7000 + T]
        share_i = nodes_flat[0:1, 11000:11000 + T].bitcast(I32)
        share = nodes_flat[0:1, 3300:3300 + T]
        gb = sb("gb", [P, 4 * D])
        fl = sb("fl", [P, 4])
        fl_i = sb("fl_i", [1, 2], I32)
        epsc = sb("epsc", [P, 1])
        zeros = sb("zeros", [P, R])

        xb = Gx[:, :, 0:2, :]
        xm = CTx[:, 0:8 * P].rearrange("p (s a n) -> p s a n", s=2, a=2)
        gin = rings[:, 0:2048].rearrange("p (s a f) -> p s a f", s=2, a=2)
        rz = rings[:, 2048:3072].rearrange("p (s a f) -> p s a f", s=2, a=2)
        wide = rings[:, 2 * J * D:2 * J * D + J * WIDE].rearrange("p (j w) -> p j w", j=J)
        assert J * WIDE <= 2 * J * D
        bn = rings[:, 3100:3100 + NB * 6].rearrange("p (b k) -> p b k", k=6)
        assert 3100 + NB * 6 <= 3712
        x1s = rings[:, 3712:3712 + 4 * D].rearrange("p (s a d) -> p s a d", s=2, a=2)
        h_flat = h[:, :, :, :].rearrange("p s j d -> p (s j d)")
        xa, xr, zt, x1t = (h_flat[0:R, k * D:(k + 1) * D] for k in range(4))
        yT, hT, x1T = (h_flat[:, 4 * D + k * R:4 * D + (k + 1) * R] for k in range(3))
        PQ = h_flat[0:R, 6 * D:8 * D]
        st = h_flat[0:R, 8 * D:8 * D + 16]
        assert 3 * R <= 2 * D
        nn = h_flat[:, 0:4 * D].rearrange("p (s a d) -> p s a d", s=2, a=2)
        dd = h_flat[:, 4 * D:8 * D].rearrange("p (s a d) -> p s a d", s=2, a=2)

        hp = [ps(f"hp{i}", [P, 1024]) for i in range(2)]
        cp = ps("cp", [P, 1024])
        up = ps("up", [P, 512])
        vp = ps("vp", [P, 512])

        s = {}

        def S(name):
            if name not in s:
                s[name] = sem(name)
            return s[name]

        class Step:
            def __init__(self, static, i=None):
                self.static, self.i = static, i

            def back(self, lag):
                return Step(self.static - lag, self.i)

            @property
            def t(self):
                return self.static if self.i is None else self.i * U + self.static

            @property
            def slot(self):
                return self.static % U

            @property
            def lap(self):
                return self.static // U if self.i is None else self.i + self.static // U

            def since(self, first):
                return self.i is not None or self.static >= first

            def within(self, count):
                return self.i is not None or 0 <= self.static < count

        def turns(eng, count, lag, body, top=None, peel=2 * U):
            for k in range(peel):
                body(Step(k), None)
            n = (count - peel) // U
            with eng.Fori(0, n) as i:
                loaded = top(Step(peel, i)) if top else None
                for k in range(U):
                    body(Step(peel + k, i), loaded[k] if loaded else None)
            for k in range(peel + n * U, count + lag):
                body(Step(k), None)

        def settled(eng):
            eng.sem_inc(S("settled"), 1)

        def flag(eng):
            eng.wait_ge(S("flag_ready"), 1)
            return eng.value_load(fl_i[0:1, 0:1], min_val=0, max_val=1)


        def bases(eng, regs, t):
            eng.load(regs, base_i[0:1, bass.ds(t.t + OFF, U)])
            return [eng.snap(r, min_val=0, max_val=N - 1) for r in regs]

        def one_base(eng, t):
            return eng.value_load(base_i[0:1, t.t + OFF:t.t + OFF + 1], min_val=0, max_val=N - 1)

        def blocks(t):
            return bass.ds(t.t * 2, 2)

        class Tile:
            def __init__(self, n, first, last):
                self.n, self.first, self.last = n, first, last

            @property
            def rows(self):
                return N - (NT - 1) * R if self.last else R

        def due(t, lag):
            b = t.back(lag)
            if b.slot or (b.i is None and not 0 <= b.lap < NT):
                return None
            return Tile(b.lap, b.i is None and b.lap == 0, b.i is None and b.lap == NT - 1)

        def tiles(eng, body):
            body(Tile(0, True, False))
            with eng.Fori(1, NT - 1) as n:
                body(Tile(n, False, False))
            body(Tile(NT - 1, False, True))

        def cols(t):
            return bass.ds(t.t * (2 * P), 2 * P)

        def hslots(k):
            return [512 * (j // 3) + (D + 1) * (j % 3) for j in range(J)]

        Y0 = (U - 1) + 4 + SLACK
        LAG0, LAG1 = Y0 + 7, 8
        PEEL0 = -(-LAG0 // U) * U
        NPEEL = 4
        HS = hslots(0)
        consts = []

        def row(v):
            return v.rearrange("(a d) -> a d", a=1)

        def col(v):
            return v.rearrange("(d a) -> d a", a=1)

        consts += [
            (W1[:, :], L0_gnn_W1), (W2[:, :], L0_gnn_W2), (b1c[:, :], col(L0_gnn_b1)),
            (b2bc[:, :], row(L0_gnn_b2).to_broadcast([P, D])),
            (eps1[:, 0:1], row(L0_gnn_eps).to_broadcast([P, 1])),
            (Wab[:, 0, :], L1_gnn_W1[0:D, :]), (Wab[:, 1, :], L1_gnn_W1[D:2 * D, :]),
            (W3g[:, :], L1_gnn_W1[2 * D:2 * D + ED, :]),
            (b1bc[:, :], row(L1_gnn_b1).to_broadcast([P, D])),
            (g_bc[:, :], row(L1_gnn_ln_g).to_broadcast([P, D])),
            (b_bc[:, :], row(L1_gnn_ln_b).to_broadcast([P, D])),
            (lnb_c[:, :], col(L1_gnn_ln_b)), (V2[:, :], L1_gnn_W2), (b2row[:, 0, :], row(L1_gnn_b2)),
            (gbias[:, 0:1], row(L1_gnn_gate_b).to_broadcast([P, 1])),
            (Wg[:, 0, :, :], L1_gnn_W_ih.rearrange("(c p) d -> p c d", p=P)),
            (Wg[:, 1, :, :], L1_gnn_W_hh.rearrange("(c p) d -> p c d", p=P)),
            (bi[:, :], row(L1_gnn_b_ih).to_broadcast([P, 3 * D])),
            (bh[:, :], row(L1_gnn_b_hh).to_broadcast([P, 3 * D])),
        ] + [(rhs[0:ED, k, D:D + 1], L1_gnn_gate_w) for k in range(U)]

        block = ctx.enter_context(nc.Block())

        @block.sync
        def _(sp):
            with nc.allow_non_contiguous_dma(reason="small tables"):
                sp.dma_start(aggT[0:FR, 0:FG * G].bitcast(I32),
                             dst.rearrange("(p f) -> p f", p=FR)).then_inc(S("dst_all"), 16)
                sp.dma_start(base_i[0:1, OFF:OFF + T],
                             dst.rearrange("(a t f) -> a t f", a=1, f=G)[:, :, 0]).then_inc(S("base_loaded"), 16)
                for to, frm in consts:
                    sp.dma_start(to, frm).then_inc(S("consts"), 16)
            general = flag(sp)

            def load_group(layer, t):
                if t.since(U):
                    sp.wait_ge(S(f"gathered{layer}_{t.slot}"), t.lap * (16 * J))
                sp.dma_start(idx[:, t.slot, :], src_v[t.t, :, :]).then_inc(S(f"idx{layer}_{t.slot}"), 16)
                if t.since(U):
                    sp.wait_ge(S(f"onehot{layer}"), t.t - (U - 1))
                sp.dma_start(dsti[:, t.slot, :], dst_v[t.t, :, :]).then_inc(S(f"dst{layer}_{t.slot}"), 16)

            def load_x(q, to, name, used):
                if not q.first:
                    sp.wait_ge(S(used), q.n)
                sp.dma_start(to[0:q.rows, :], x[bass.ds(q.n * R, q.rows), :]).then_inc(S(name), 16)

            def store_x1(q):
                sp.wait_ge(S("x1_made"), q.n + 1)
                sp.dma_start(X1D[bass.ds(q.n * R, R), :], x1t).then_inc(S("x1_stored"), 16)

            def store_pq(q):
                sp.wait_ge(S("pq_made"), q.n + 1)
                for a, to in enumerate((PD, QD)):
                    sp.dma_start(to[bass.ds(q.n * R, R), :], PQ[:, a * D:(a + 1) * D]).then_inc(S("pq_stored"), 16)

            with sp.If(general == 0):
                def body(t, base):
                    if t.within(T):
                        load_group(0, t)
                    if due(t, Y0 - 2):
                        load_x(due(t, Y0 - 2), xa, "xa_loaded", "x_turned")
                    if due(t, Y0):
                        load_x(due(t, Y0), xr, "xr_loaded", "z_made")
                    if due(t, Y0 + 4):
                        store_x1(due(t, Y0 + 4))
                    if due(t, Y0 + 6):
                        store_pq(due(t, Y0 + 6))
                turns(sp, T, LAG0, body, peel=PEEL0)
            with sp.Else():
                with sp.Fori(0, T) as t:
                    sp.wait_ge(S("g_summed0"), t + 1)
                    sp.dma_start(idx[:, 0, :], src_v[t, :, :]).then_inc(S("g_idx0"), 16)
                    sp.dma_start(dsti[:, 0, :], dst_v[t, :, :]).then_inc(S("g_idx0"), 16)

                def body(q):
                    load_x(q, xa, "xa_loaded", "x_turned")
                    load_x(q, xr, "xr_loaded", "z_made")
                    store_x1(q)
                    store_pq(q)
                tiles(sp, body)
            sp.wait_ge(S("x1_stored"), 16 * NT)
            sp.wait_ge(S("pq_stored"), 32 * NT)

            XB = 7
            assert NB % XB == 0 and XB <= 2 * U

            def load_x1(k):
                n = NB // XB
                sp.dma_start(nodes[:, k * n:(k + 1) * n, :],
                             X1D[k * n * P:(k + 1) * n * P, :].rearrange("(b p) d -> p b d", p=P)).then_inc(S("x1_back"), 16)

            with sp.If(general == 0):
                def body(t, base):
                    if not t.within(T):
                        return
                    load_group(1, t)
                    if t.since(U):
                        sp.wait_ge(S("tile_turned"), t.t - (U - 1))
                    sp.dma_start(Ce[:, t.slot, :, 0:ED], ef_v[t.t, :, :, :]).then_inc(S(f"ef_{t.slot}"), 16)
                    if t.since(U):
                        sp.wait_ge(S("h_made"), t.t - (U - 1))
                    if base is None:
                        base = one_base(sp, t)
                    sp.dma_start(rhs[ED:C, t.slot, 0:D], QD[bass.ds(base, W), :]).then_inc(S(f"win_{t.slot}"), 16)
                    if t.i is None and t.static < XB:
                        load_x1(t.static)
                regs = [sp.alloc_register(f"sp_base{k}") for k in range(U)]
                turns(sp, T, 0, body, top=lambda t: bases(sp, regs, t))
            with sp.Else():
                for k in range(XB):
                    load_x1(k)
                with sp.Fori(0, T) as t:
                    sp.wait_ge(S("g_summed1"), t + 1)
                    sp.dma_start(idx[:, 0, :], src_v[t, :, :]).then_inc(S("g_idx1"), 16)
                    sp.dma_start(dsti[:, 0, :], dst_v[t, :, :]).then_inc(S("g_idx1"), 16)
                    sp.dma_start(idx2[:, :], dst_v[t, :, :]).then_inc(S("g_idx1"), 16)
                    sp.dma_start(Ce[:, 3, :, 0:ED], ef_v[t, :, :, :]).then_inc(S("g_idx1"), 16)

            def body(t, _):
                sp.wait_ge(S("out_made"), t.t + 1)
                last = t.i is None and t.static == NC - 1
                for a in range(2):
                    n = min(P, N - (NC - 1) * 2 * P - a * P) if last else P
                    sp.dma_start(out[bass.ds(t.t * (2 * P) + a * P, n), :],
                                 xb[0:n, t.slot, a, :]).then_inc(S(f"stored_{t.slot}"), 16)
            turns(sp, NC, 0, body, peel=NPEEL)
            for k in range(U):
                sp.wait_ge(S(f"stored_{k}"), 32 * len(range(k, NC, U)))

        @block.gpsimd
        def _(pool):
            pool.iota(iota_i[:, :], pattern=[[1, WIDE]], base=0, channel_multiplier=0).then_inc(S("iota_made"), 1)
            pool.iota(share_i[:, :], pattern=[[R // U, T]], base=0, channel_multiplier=0).then_inc(S("iota_made"), 1)
            pool.memset(ones[:, :], 1.0).then_inc(S("ones_made"), 1)
            pool.wait_ge(S("ones_made"), 1)
            pool.affine_select(out=ident[:, :], in_=ones[:, :], compare_op=ALU.is_equal, fill=0.0, base=0,
                               pattern=[[1, P]], channel_multiplier=-1).then_inc(S("ident_made"), 1)
            general = flag(pool)

            def gather(to, table, index, name):
                settled(pool)
                for j in range(J):
                    pool.indirect_dma_start(to[:, j, :], None, table,
                                            bass.IndirectOffsetOnAxis(ap=index[:, j:j + 1], axis=0)).then_inc(S(name), 16)

            for layer, table in ((0, x), (1, PD)):
                if layer:
                    pool.wait_ge(S("pq_stored"), 32 * NT)
                with pool.If(general == 0):
                    def body(t, _):
                        pool.wait_ge(S(f"idx{layer}_{t.slot}"), (t.lap + 1) * 16)
                        if t.since(U):
                            pool.wait_ge(S("h_added" if layer else "sums_made0"), t.t - (U - 1))
                        gather(Gx[:, t.slot], table, idx[:, t.slot], f"gathered{layer}_{t.slot}")
                    turns(pool, T, 0, body)
                with pool.Else():
                    with pool.Fori(0, T) as t:
                        pool.wait_ge(S(f"g_idx{layer}"), (t + 1) * (64 if layer else 32))
                        gather(Gx[:, 0], table, idx[:, 0], f"g_gathered{layer}")
                        if layer:
                            gather(Gx[:, 1], QD, idx2, f"g_gathered{layer}")

        @block.tensor
        def _(pe):
            pe.wait_ge(S("ident_made"), 1)
            pe.wait_ge(S("range_rows"), 1)
            pe.matmul(up[0:1, 0:FR], fl[0:FR, 2:3], ident[0:FR, 0:FR], start=True, stop=True).then_inc(S("range_row"), 1)
            pe.wait_ge(S("base_float"), 1)
            for a, n in ((0, 512), (512, T - 512)):
                mm = pe.matmul(cp[:, a:a + n], ones[0:1, :], base_f[0:1, a:a + n], start=True, stop=True)
            mm.then_inc(S("base_spread"), 1)
            pe.wait_ge(S("consts"), 16 * len(consts))
            for a in range(2):
                for k in range(3):
                    mm = pe.transpose(hp[a][:, k * P:(k + 1) * P], Wg[:, a, k, :], ident[:, :])
            mm.then_inc(S("gru_turned"), 1)
            pe.matmul(hp[0][0:1, 512:512 + D], lnb_c[:, :], V2[:, :], start=True, stop=True).then_inc(S("b2_made"), 1)
            general = flag(pe)

            def window_sums(layer, t):
                pe.wait_ge(S("msg_made" if layer else "onehot0"), t.t + 1)
                if not layer:
                    pe.wait_ge(S(f"gathered0_{t.slot}"), (t.lap + 1) * (16 * J))
                if t.since(1):
                    pe.wait_ge(S(f"sums_copied{layer}"), t.t)
                for j in range(J):
                    if layer:
                        mm = pe.matmul(up[0:W, 0:M], Sg[:, t.slot % 2, j, :], msg[:, t.slot % 2, j, :],
                                       start=(j == 0), stop=(j == J - 1))
                    else:
                        mm = pe.matmul(up[0:W, 0:D], Ce[:, t.slot, j, ED:C], Gx[:, t.slot, j, :],
                                       start=(j == 0), stop=(j == J - 1))
                mm.then_inc(S(f"sums_made{layer}"), 1)

            def turn_sums(layer, t):
                pe.wait_ge(S(f"sums_copied{layer}"), t.t + 1)
                if t.since(1):
                    pe.wait_ge(S(f"added{layer}"), t.t)
                settled(pe)
                mm = pe.transpose(vp[:, 0:W], Us[:, 0:D], ident[0:W, 0:W])
                if layer:
                    mm = pe.transpose(vp[0:1, W:2 * W], Us[:, D:M], ident[0:W, 0:W])
                mm.then_inc(S(f"sums_turned{layer}"), 1)

            def turn_x(q):
                pe.wait_ge(S("xa_loaded"), (q.n + 1) * 16)
                if not q.first:
                    pe.wait_ge(S("y_made"), q.n)
                settled(pe)
                pe.transpose(cp[:, 0:R], xa, ident[0:R, 0:R]).then_inc(S("x_turned"), 1)

            def hidden(q):
                pe.wait_ge(S("y_made"), q.n + 1)
                if not q.first:
                    pe.wait_ge(S("hidden_made"), q.n)
                settled(pe)
                pe.matmul(cp[:, 512:512 + R], W1[:, :], yT, start=True, stop=True).then_inc(S("hidden_mm"), 1)

            def mlp(q):
                pe.wait_ge(S("hidden_made"), q.n + 1)
                if not q.first:
                    pe.wait_ge(S("z_made"), q.n)
                settled(pe)
                pe.matmul(hp[0][0:R, 0:D], hT, W2[:, :], start=True, stop=True).then_inc(S("mlp_mm"), 1)

            def turn_x1(q):
                pe.wait_ge(S("x1_made"), q.n + 1)
                if not q.first:
                    pe.wait_ge(S("x1T_copied"), q.n)
                settled(pe)
                pe.transpose(hp[0][:, 512:512 + R], x1t, ident[0:R, 0:R]).then_inc(S("x1_turned"), 1)

            def pq(q):
                pe.wait_ge(S("x1T_copied"), q.n + 1)
                if not q.first:
                    pe.wait_ge(S("pq_made"), q.n)
                settled(pe)
                pe.matmul(hp[1][0:R, 0:2 * D], x1T, Wabc[:, :, :], start=True, stop=True).then_inc(S("pq_mm"), 1)

            pe.wait_ge(S("base_saved"), 1)
            with pe.If(general == 0):
                def body(t, _):
                    if t.back(2).within(T):
                        window_sums(0, t.back(2))
                    if t.back(3).within(T):
                        turn_sums(0, t.back(3))
                    if due(t, Y0 - 1):
                        turn_x(due(t, Y0 - 1))
                    if due(t, Y0):
                        hidden(due(t, Y0))
                    if due(t, Y0 + 1):
                        mlp(due(t, Y0 + 1))
                    if due(t, Y0 + 3):
                        turn_x1(due(t, Y0 + 3))
                    if due(t, Y0 + 4):
                        pq(due(t, Y0 + 4))
                turns(pe, T, LAG0, body, peel=PEEL0)
            with pe.Else():
                with pe.Fori(0, T) as t:
                    with pe.Fori(0, NW) as w:
                        pe.wait_ge(S("g_gathered0"), (t + 1) * (16 * J))
                        pe.wait_ge(S("g_wide0"), t * NW + w + 1)
                        for j in range(J):
                            mm = pe.matmul(cp[:, 0:WIDE], Gx[:, 0, j, :], wide[:, j, :], start=(j == 0), stop=(j == J - 1))
                        mm.then_inc(S("g_sums0"), 1)

                def body(q):
                    turn_x(q)
                    hidden(q)
                    mlp(q)
                    turn_x1(q)
                    pq(q)
                tiles(pe, body)
            pe.wait_ge(S("pq_made"), NT)

            with pe.If(general == 0):
                def body(t, _):
                    b, c = t.back(1), t.back(2)
                    if b.within(T):
                        pe.wait_ge(S("onehot1"), b.t + 1)
                        pe.wait_ge(S(f"ef_{b.slot}"), (b.lap + 1) * 16)
                        if b.since(1):
                            pe.wait_ge(S("tile_copied"), b.t)
                        for j in range(J):
                            mm = pe.transpose(cp[0:C, j * P:(j + 1) * P], Ce[:, b.slot, j, :], ident[:, :])
                        mm.then_inc(S("tile_turned"), 1)
                    if c.within(T):
                        pe.wait_ge(S("tile_copied"), c.t + 1)
                        pe.wait_ge(S(f"win_{c.slot}"), (c.lap + 1) * 16)
                        if c.since(2):
                            pe.wait_ge(S("h_added"), c.t - 1)
                            pe.wait_ge(S("ge_made"), c.t - 1)
                        for j in range(J):
                            mm = pe.matmul(hp[c.slot % 2][:, HS[j]:HS[j] + D + 1], CT[:, c.slot % 2, j * P:(j + 1) * P],
                                           rhs[:, c.slot, :], start=True, stop=True)
                        mm.then_inc(S("h_made"), 1)
                    if t.back(6).within(T):
                        turn_sums(1, t.back(6))
                    if t.back(5).within(T):
                        window_sums(1, t.back(5))
                turns(pe, T, LAG1, body)
            with pe.Else():
                with pe.Fori(0, T) as t:
                    pe.wait_ge(S("g_idx1"), (t + 1) * 64)
                    settled(pe)
                    for j in range(J):
                        mm = pe.transpose(cp[0:ED, j * P:(j + 1) * P], Ce[:, 3, j, 0:ED], ident[:, :])
                    mm.then_inc(S("g_turned"), 1)
                    pe.wait_ge(S("g_copied"), t + 1)
                    for j in range(J):
                        mm = pe.matmul(hp[0][:, HS[j]:HS[j] + D + 1], CT[0:ED, 0, j * P:(j + 1) * P],
                                       rhs[0:ED, 0, :], start=True, stop=True)
                    mm.then_inc(S("g_h_made"), 1)
                    with pe.Fori(0, NW) as w:
                        pe.wait_ge(S("g_wide1"), t * NW + w + 1)
                        for j in range(J):
                            pe.matmul(cp[:, 0:WIDE], msg[:, 0, j, 0:D], wide[:, j, :], start=(j == 0), stop=(j == J - 1))
                        for j in range(J):
                            mm = pe.matmul(cp[0:1, 512:512 + WIDE], msg[:, 0, j, D:M], wide[:, j, :], start=(j == 0), stop=(j == J - 1))
                        mm.then_inc(S("g_sums1"), 1)

            pe.wait_ge(S("layer1_summed"), 1)

            def body(t, _):
                if t.within(NC):
                    if t.since(2):
                        pe.wait_ge(S("xm_copied"), t.t - 1)
                    pe.wait_ge(S("x1_placed"), t.t + 1)
                    o = 512 * (t.slot % 2)
                    for a in range(2):
                        pe.transpose(cp[:, o + a * P:o + (a + 1) * P], x1s[:, t.slot % 2, a, :], ident[:, :])
                    pe.matmul(cp[:, o + 2 * P:o + 4 * P], V2[:, :], aggT[:, cols(t)], start=True, stop=False)
                    pe.matmul(cp[:, o + 2 * P:o + 4 * P], b2row[0:1, 1, :], gsum[0:1, cols(t)],
                              start=False, stop=True).then_inc(S("xm_mm"), 1)
                b = t.back(1)
                if b.within(NC):
                    pe.wait_ge(S("xm_copied"), b.t + 1)
                    if b.since(2):
                        pe.wait_ge(S("gin_made"), b.t - 1)
                    for a in range(2):
                        to = hp[b.slot % 2][:, 512 * a:512 * (a + 1)]
                        x1T = xm[:, b.slot % 2, 0, a * P:(a + 1) * P]
                        mT = xm[:, b.slot % 2, 1, a * P:(a + 1) * P]
                        pe.matmul(to[:, 0:2 * D], mT, WgT[:, 0, 0:2 * D], start=True, stop=False)
                        pe.matmul(to[:, 0:2 * D], x1T, WgT[:, 1, 0:2 * D], start=False, stop=True)
                        pe.matmul(to[:, 2 * D:3 * D], mT, WgT[:, 0, 2 * D:3 * D], start=True, stop=True)
                        mm = pe.matmul(to[:, 3 * D:4 * D], x1T, WgT[:, 1, 2 * D:3 * D], start=True, stop=True)
                    mm.then_inc(S("gru_mm"), 1)
            turns(pe, NC, 2, body, peel=NPEEL)

        @block.scalar
        def _(act):
            general = flag(act)

            def copy_sums(layer, t):
                act.wait_ge(S(f"sums_made{layer}"), t.t + 1)
                if t.since(1):
                    act.wait_ge(S(f"sums_turned{layer}"), t.t)
                n = M if layer else D
                act.activation(Us[:, 0:n], up[0:W, 0:n], ACT.Copy).then_inc(S(f"sums_copied{layer}"), 1)

            def relu(q):
                act.wait_ge(S("hidden_mm"), q.n + 1)
                if not q.first:
                    act.wait_ge(S("mlp_mm"), q.n)
                act.activation(hT, cp[:, 512:512 + R], ACT.Relu, bias=b1c[:, 0:1]).then_inc(S("hidden_made"), 1)

            def root(q):
                act.wait_ge(S("var_z"), q.n + 1)
                act.activation(st[:, 9:10], st[:, 8:9], ACT.Sqrt).then_inc(S("std_z"), 1)

            def copy_x1T(q):
                act.wait_ge(S("x1_turned"), q.n + 1)
                if not q.first:
                    act.wait_ge(S("pq_mm"), q.n)
                act.activation(x1T, hp[0][:, 512:512 + R], ACT.Copy).then_inc(S("x1T_copied"), 1)

            with act.If(general == 0):
                def body(t, _):
                    if t.back(2).within(T):
                        copy_sums(0, t.back(2))
                    if due(t, Y0 + 1):
                        relu(due(t, Y0 + 1))
                    if due(t, Y0 + 2):
                        root(due(t, Y0 + 2))
                    if due(t, Y0 + 4):
                        copy_x1T(due(t, Y0 + 4))
                turns(act, T, LAG0, body, peel=PEEL0)
            with act.Else():
                def body(q):
                    relu(q)
                    root(q)
                    copy_x1T(q)
                tiles(act, body)

            def std(n):
                act.wait_ge(S("var_made"), n)
                act.activation(rtmp[:, :], rvar[:, :], ACT.Sqrt).then_inc(S("std_made"), 1)

            def gate_exp(k, name):
                for lo, hi in ((0, 3), (3, J)):
                    a = act.activation(ge[:, k, lo:hi].unsqueeze(2),
                                       hp[k][:, HS[lo]:HS[lo] + (hi - lo) * (D + 1)].rearrange("p (j f) -> p j f", f=D + 1)[:, :, D:D + 1],
                                       ACT.Exp, scale=-1.0, bias=gbias[:, 1:2])
                a.then_inc(S(name), 1)

            def guess(k, sums, logs, name, n):
                for j in range(J):
                    a = act.activation(sq[:, j, :], h[:, k, j, :], ACT.Square, accum_out=ss[:, k, j:j + 1])
                a.then_inc(S(sums), 1)
                act.wait_ge(S(sums), n)
                act.activation(lnv[:, k, :], ss[:, k, :], ACT.Ln, scale=1.0 / D, bias=epsc[:, 0:1]).then_inc(S(logs), 1)
                act.wait_ge(S(logs), n)
                act.activation(r0[:, k, :], lnv[:, k, :], ACT.Exp, scale=-0.5).then_inc(S(name), 1)

            act.preload_act_table_set("natural_log_exp_and_others")
            with act.If(general == 0):
                def body(t, _):
                    b, c = t.back(1), t.back(3)
                    if c.within(T):
                        act.wait_ge(S("h_made"), c.t + 1)
                        if c.since(2):
                            act.wait_ge(S("msg_made"), c.t - 1)
                        gate_exp(c.slot % 2, "ge_made")
                    if t.back(6).within(T):
                        copy_sums(1, t.back(6))
                    if b.within(T):
                        act.wait_ge(S("tile_turned"), b.t + 1)
                        if b.since(2):
                            act.wait_ge(S("h_made"), b.t - 1)
                        act.activation(CT[:, b.slot % 2, :], cp[0:C, 0:J * P], ACT.Copy).then_inc(S("tile_copied"), 1)
                    if c.within(T):
                        act.wait_ge(S("h_added"), c.t + 1)
                        if c.since(1):
                            act.wait_ge(S("squares"), c.t)
                        guess(c.slot % 2, "squares", "logs", "r0_made", c.t + 1)
                turns(act, T, LAG1, body)
            with act.Else():
                with act.Fori(0, T) as t:
                    act.wait_ge(S("g_turned"), t + 1)
                    act.activation(CT[0:ED, 0, :], cp[0:ED, 0:J * P], ACT.Copy).then_inc(S("g_copied"), 1)
                    act.wait_ge(S("g_h_made"), t + 1)
                    gate_exp(0, "g_ge_made")
                    act.wait_ge(S("g_h_added"), t + 1)
                    guess(0, "g_squares", "g_logs", "g_r0_made", t + 1)

            act.wait_ge(S("layer1_summed"), 1)
            act.wait_ge(S("x1_back"), 16 * (7))

            def body(t, _):
                if t.within(NC):
                    k = t.slot % 2
                    if t.since(2):
                        act.wait_ge(S("xm_mm"), t.t - 1)
                    act.activation(x1s[:, k], nodes[:, blocks(t), :], ACT.Copy).then_inc(S("x1_placed"), 1)
                    act.wait_ge(S("xm_mm"), t.t + 1)
                    if t.since(2):
                        act.wait_ge(S("gru_mm"), t.t - 1)
                    act.activation(xm[:, k], cp[:, 512 * k:512 * (k + 1)].rearrange("p (a n) -> p a n", a=2), ACT.Copy).then_inc(S("xm_copied"), 1)
                b = t.back(2)
                if b.within(NC):
                    k = b.slot % 2
                    act.wait_ge(S("gin_made"), b.t + 1)
                    if b.since(2):
                        act.wait_ge(S("z2_made"), b.t - 1)
                    act.activation(rz[:, k], gin[:, k, :, 0:2 * D], ACT.Sigmoid).then_inc(S("rz_made"), 1)
                c = t.back(3)
                if c.within(NC):
                    k = c.slot % 2
                    act.wait_ge(S("n_in"), c.t + 1)
                    act.activation(nn[:, k], nn[:, k], ACT.Tanh).then_inc(S("n_made"), 1)
            turns(act, NC, 4, body, peel=NPEEL)
            std(1)

        @block.vector
        def _(v):
            v.wait_ge(S("dst_all"), 16)
            allv = aggT[0:FR, 0:FG * G].bitcast(I32).rearrange("p (g f) -> p g f", f=G)
            relv = nodes[:, :, :].rearrange("p b d -> p (b d)")[0:FR, 0:FG * G].rearrange("p (g f) -> p g f", f=G)
            v.tensor_tensor(relv, allv, allv[:, :, 0:1].to_broadcast([FR, FG, G]), ALU.subtract).then_inc(S("rel"), 1)
            v.wait_ge(S("rel"), 1)
            v.tensor_reduce(fl[0:FR, 0:1], relv, AX.XY, ALU.max)
            v.tensor_reduce(fl[0:FR, 1:2], relv, AX.XY, ALU.min).then_inc(S("rel"), 1)
            v.wait_ge(S("rel"), 2)
            v.tensor_scalar(fl[0:FR, 3:4], fl[0:FR, 0:1], float(-(W - 1)), None, ALU.add).then_inc(S("rel"), 1)
            v.wait_ge(S("rel"), 3)
            v.scalar_tensor_tensor(fl[0:FR, 2:3], fl[0:FR, 1:2], -1.0, fl[0:FR, 3:4], ALU.mult, ALU.max).then_inc(S("range_rows"), 1)
            v.wait_ge(S("base_loaded"), 16)
            v.tensor_copy(base_f[:, :], base_i[0:1, OFF:OFF + T]).then_inc(S("base_float"), 1)
            v.wait_ge(S("range_row"), 1)
            v.wait_ge(S("iota_made"), 2)
            v.tensor_copy(share[:, :], share_i[:, :]).then_inc(S("rel"), 1)
            v.wait_ge(S("rel"), 4)
            v.wait_ge(S("base_float"), 1)
            v.tensor_tensor(share[:, :], share[:, :], base_f[:, :], ALU.subtract)
            v.tensor_reduce(rtmp[0:1, 0:1], up[0:1, 0:FR], AX.X, ALU.max).then_inc(S("rel"), 1)
            v.wait_ge(S("rel"), 5)
            v.tensor_reduce(rtmp[0:1, 1:2], share[:, :], AX.X, ALU.max).then_inc(S("rel"), 1)
            v.wait_ge(S("rel"), 6)
            v.scalar_tensor_tensor(rtmp[0:1, 2:3], rtmp[0:1, 1:2], float(-SLACK * (R // U)), rtmp[0:1, 0:1], ALU.add, ALU.max).then_inc(S("rel"), 1)
            v.wait_ge(S("rel"), 7)
            v.tensor_scalar(fl_i[0:1, 0:1], rtmp[0:1, 2:3], 0.0, None, ALU.is_gt).then_inc(S("flag_ready"), 1)
            v.wait_ge(S("base_spread"), 1)
            v.tensor_copy(base_bc[:, :], cp[:, 0:T])
            v.wait_ge(S("iota_made"), 1)
            v.tensor_copy(iota[:, :], iota_i[:, :])
            v.memset(aggT[:, :], 0.0)
            v.memset(gsum[:, :], 0.0).then_inc(S("base_saved"), 1)
            v.wait_ge(S("base_saved"), 1)
            general = flag(v)

            v.wait_ge(S("consts"), 16 * len(consts))
            steps = [0]

            def step(ins):
                steps[0] += 1
                ins.then_inc(S("tables"), 1)

            def after():
                v.wait_ge(S("tables"), steps[0])
            v.tensor_scalar(eps1[:, 1:2], eps1[:, 0:1], 1.0, None, ALU.add)
            v.memset(epsc[:, :], LN_EPS)
            v.memset(zeros[:, :], 0.0)
            v.memset(msg[:, :, :, D:M], 1.0)
            v.memset(q_bias[:, 0:D], 0.0)
            for k in range(U):
                v.memset(rhs[ED:C, k, D:D + 1], 0.0)
            v.tensor_scalar(gbias[:, 1:2], gbias[:, 0:1], -1.0, None, ALU.mult)
            v.tensor_scalar(nb_bc[:, :], b_bc[:, :], -1.0, None, ALU.mult)
            v.tensor_tensor(gb[:, 0:2 * D], bi[:, 0:2 * D], bh[:, 0:2 * D], ALU.add)
            v.tensor_copy(gb[:, 2 * D:3 * D], bi[:, 2 * D:3 * D])
            v.tensor_copy(gb[:, 3 * D:4 * D], bh[:, 2 * D:3 * D])
            v.wait_ge(S("gru_turned"), 1)
            for a in range(2):
                v.tensor_copy(WgT[:, a, :], hp[a][:, 0:3 * D])
            v.wait_ge(S("b2_made"), 1)
            v.tensor_tensor(b2row[0:1, 1, :], b2row[0:1, 0, :], hp[0][0:1, 512:512 + D], ALU.add)
            v.tensor_reduce(wmean[:, 0:2], Wab[:, :, :], AX.X, ALU.add)
            v.tensor_reduce(wmean[0:ED, 2:3], W3g[:, :], AX.X, ALU.add)
            step(v.tensor_reduce(wmean[:, 3:4], b1bc[:, :], AX.X, ALU.add))
            after()
            step(v.tensor_scalar(wmean[:, 4:6], wmean[:, 0:2], -1.0 / D, None, ALU.mult))
            step(v.tensor_scalar(wmean[0:ED, 6:7], wmean[0:ED, 2:3], -1.0 / D, None, ALU.mult))
            step(v.tensor_scalar(wmean[:, 7:8], wmean[:, 3:4], -1.0 / D, None, ALU.mult))
            after()
            for a in range(2):
                v.tensor_scalar(Wabc[:, a, :], Wab[:, a, :], wmean[:, 4 + a:5 + a], None, ALU.add)
            for k in range(U):
                v.tensor_scalar(rhs[0:ED, k, 0:D], W3g[:, :], wmean[0:ED, 6:7], None, ALU.add)
            step(v.tensor_scalar(q_bias[:, D:2 * D], b1bc[:, :], wmean[:, 7:8], None, ALU.add))
            after()

            def onehot(layer, t):
                v.wait_ge(S(f"dst{layer}_{t.slot}"), (t.lap + 1) * 16)
                if t.since(1):
                    v.wait_ge(S(f"onehot{layer}"), t.t)
                v.tensor_scalar(drel[:, t.slot, :], dsti[:, t.slot, :], base_bc[:, t.t:t.t + 1] if t.i is None else base_bc[:, bass.ds(t.t, 1)],
                                None, ALU.subtract).then_inc(S(f"drel{layer}"), 1)
                if layer:
                    yield
                v.wait_ge(S(f"drel{layer}"), t.t + 1)
                if t.since(U):
                    v.wait_ge(S("tile_turned" if layer else "sums_made0"), t.t - (U - 1))
                if layer and t.since(U):
                    v.wait_ge(S("Sg_made"), t.t - (U - 1))
                v.tensor_tensor(Ce[:, t.slot, :, ED:C], iota[:, None, 0:W].to_broadcast([P, J, W]),
                                drel[:, t.slot, :, None].to_broadcast([P, J, W]), ALU.is_equal).then_inc(S(f"onehot{layer}"), 1)

            def add(layer, t, base):
                if base is None:
                    base = one_base(v, t)
                v.wait_ge(S(f"sums_turned{layer}"), t.t + 1)
                if t.since(1):
                    v.wait_ge(S(f"added{layer}"), t.t)
                a = v.tensor_tensor(aggT[:, bass.ds(base, W)], aggT[:, bass.ds(base, W)], vp[:, 0:W], ALU.add)
                if layer:
                    a = v.tensor_tensor(gsum[0:1, bass.ds(base, W)], gsum[0:1, bass.ds(base, W)], vp[0:1, W:2 * W], ALU.add)
                a.then_inc(S(f"added{layer}"), 1)

            def add_wide(layer, t):
                v.tensor_copy(drel[:, 0, :], dsti[:, 0, :]).then_inc(S(f"g_drel{layer}"), 1)
                with v.Fori(0, NW) as w:
                    v.wait_ge(S(f"g_drel{layer}"), t * (NW + 1) + w + 1)
                    for j in range(J):
                        if layer:
                            a = v.tensor_scalar(wide[:, j, :], iota[:, :], drel[:, 0, j:j + 1], gate[:, 0, j:j + 1], ALU.is_equal, ALU.mult)
                        else:
                            a = v.tensor_scalar(wide[:, j, :], iota[:, :], drel[:, 0, j:j + 1], None, ALU.is_equal)
                    a.then_inc(S(f"g_wide{layer}"), 1)
                    v.wait_ge(S(f"g_wide{layer}"), t * NW + w + 1)
                    v.tensor_scalar(drel[:, 0, :], drel[:, 0, :], float(-WIDE), None, ALU.add).then_inc(S(f"g_drel{layer}"), 1)
                    v.wait_ge(S(f"g_sums{layer}"), t * NW + w + 1)
                    to = bass.ds(w * WIDE, WIDE)
                    a = v.tensor_tensor(aggT[:, to], aggT[:, to], cp[:, 0:WIDE], ALU.add)
                    if layer:
                        a = v.tensor_tensor(gsum[0:1, to], gsum[0:1, to], cp[0:1, 512:512 + WIDE], ALU.add)
                    a.then_inc(S(f"g_added{layer}"), 1)
                v.wait_ge(S(f"g_added{layer}"), t * NW + NW)
                v.memset(fl[:, 0:1], 0.0).then_inc(S(f"g_summed{layer}"), 1)

            def y(q):
                at = bass.ds(q.n * R, R)
                v.wait_ge(S("x_turned"), q.n + 1)
                if not q.first:
                    v.wait_ge(S("hidden_mm"), q.n)
                v.scalar_tensor_tensor(yT, cp[:, 0:R], eps1[:, 1:2], aggT[:, at], ALU.mult, ALU.add).then_inc(S("y_made"), 1)
                v.wait_ge(S("y_made"), q.n + 1)
                v.tensor_tensor(aggT[:, at], zeros[:, :], zeros[:, :], ALU.add).then_inc(S("sums_cleared"), 1)

            def z(q):
                v.wait_ge(S("mlp_mm"), q.n + 1)
                v.wait_ge(S("xr_loaded"), (q.n + 1) * 16)
                v.tensor_tensor(zt, hp[0][0:R, 0:D], xr, ALU.add).then_inc(S("z_made"), 1)
                v.wait_ge(S("z_made"), q.n + 1)
                v.tensor_tensor(zt, zt, b2bc[0:R, :], ALU.add).then_inc(S("z"), 1)
                v.wait_ge(S("z"), q.n + 1)
                settled(v)
                v.bn_stats(st[:, 0:6], zt).then_inc(S("z_stats"), 1)
                v.wait_ge(S("z_stats"), q.n + 1)
                v.tensor_tensor(st[:, 6:7], st[:, 1:2], st[:, 4:5], ALU.add)
                v.tensor_tensor(st[:, 7:8], st[:, 1:2], st[:, 4:5], ALU.subtract)
                v.tensor_tensor(st[:, 8:9], st[:, 2:3], st[:, 5:6], ALU.add).then_inc(S("z_sums"), 1)
                v.wait_ge(S("z_sums"), q.n + 1)
                v.tensor_scalar(st[:, 6:7], st[:, 6:7], 0.5, None, ALU.mult)
                v.scalar_tensor_tensor(st[:, 7:8], st[:, 7:8], 0.25, st[:, 7:8], ALU.mult, ALU.mult)
                v.tensor_scalar(st[:, 8:9], st[:, 8:9], 1.0 / D, LN_EPS, ALU.mult, ALU.add).then_inc(S("z_mean"), 1)
                v.wait_ge(S("z_mean"), q.n + 1)
                v.tensor_tensor(st[:, 8:9], st[:, 8:9], st[:, 7:8], ALU.add).then_inc(S("var_z"), 1)

            def x1_rows(q):
                v.wait_ge(S("std_z"), q.n + 1)
                v.reciprocal(st[:, 10:11], st[:, 9:10]).then_inc(S("z_inv"), 1)
                v.wait_ge(S("z_inv"), q.n + 1)
                v.tensor_tensor(st[:, 11:12], st[:, 10:11], st[:, 10:11], ALU.mult).then_inc(S("z_inv2"), 1)
                v.wait_ge(S("z_inv2"), q.n + 1)
                v.scalar_tensor_tensor(st[:, 12:13], st[:, 11:12], -0.5, st[:, 8:9], ALU.mult, ALU.mult).then_inc(S("z_newton"), 1)
                v.wait_ge(S("z_newton"), q.n + 1)
                v.scalar_tensor_tensor(st[:, 13:14], st[:, 12:13], 1.5, st[:, 10:11], ALU.add, ALU.mult).then_inc(S("z_rstd"), 1)
                v.wait_ge(S("z_rstd"), q.n + 1)
                if not q.first:
                    v.wait_ge(S("x1_stored"), q.n * 16)
                    v.wait_ge(S("x1_turned"), q.n)
                v.tensor_scalar(x1t, zt, st[:, 6:7], st[:, 13:14], ALU.subtract, ALU.mult).then_inc(S("x1_made"), 1)

            def pq_rows(q):
                v.wait_ge(S("pq_mm"), q.n + 1)
                if not q.first:
                    v.wait_ge(S("pq_stored"), q.n * 32)
                v.tensor_tensor(PQ, hp[1][0:R, 0:2 * D], q_bias[0:R, :], ALU.add).then_inc(S("pq_made"), 1)

            regs = [v.alloc_register(f"dve_base{k}") for k in range(U)]
            with v.If(general == 0):
                def body(t, base):
                    if due(t, Y0):
                        v.wait_ge(S("added0"), t.t - 3 if t.i is not None else min(t.static - 3, T))
                        y(due(t, Y0))
                    if t.back(3).within(T):
                        add(0, t.back(3), base)
                    if t.within(T):
                        for _ in onehot(0, t):
                            pass
                    if due(t, Y0 + 2):
                        z(due(t, Y0 + 2))
                    if due(t, Y0 + 3):
                        x1_rows(due(t, Y0 + 3))
                    if due(t, Y0 + 5):
                        pq_rows(due(t, Y0 + 5))
                turns(v, T, LAG0, body, top=lambda t: bases(v, regs, t.back(3)), peel=PEEL0)
                v.wait_ge(S("added0"), T)
            with v.Else():
                v.memset(fl[:, 0:1], 0.0).then_inc(S("g_summed0"), 1)
                with v.Fori(0, T) as t:
                    v.wait_ge(S("g_idx0"), (t + 1) * 32)
                    v.wait_ge(S("g_summed0"), t + 1)
                    add_wide(0, t)
                v.wait_ge(S("g_summed0"), T + 1)

                def body(q):
                    y(q)
                    z(q)
                    x1_rows(q)
                    pq_rows(q)
                tiles(v, body)
            v.wait_ge(S("sums_cleared"), NT)
            v.wait_ge(S("pq_stored"), 32 * NT)

            def rows_stats(t, made):
                v.wait_ge(S(made), t.t + 1)
                settled(v)
                for a in range(2):
                    b = v.bn_stats(bn[:, bass.ds(t.t * 2 + a, 1), :], nodes[:, bass.ds(t.t * 2 + a, 1), :])
                b.then_inc(S(made + "_stats"), 1)

            def all_rstd(n, made):
                v.wait_ge(S(made + "_stats"), NC)
                v.tensor_tensor(mean[:, :], bn[:, :, 1], bn[:, :, 4], ALU.add)
                v.tensor_tensor(rtmp[:, :], bn[:, :, 1], bn[:, :, 4], ALU.subtract)
                step(v.tensor_tensor(rvar[:, :], bn[:, :, 2], bn[:, :, 5], ALU.add))
                after()
                v.tensor_scalar(mean[:, :], mean[:, :], 0.5, None, ALU.mult)
                v.scalar_tensor_tensor(rstd[:, :], rtmp[:, :], 0.25, rtmp[:, :], ALU.mult, ALU.mult)
                step(v.tensor_scalar(rvar[:, :], rvar[:, :], 1.0 / D, LN_EPS, ALU.mult, ALU.add))
                after()
                v.tensor_tensor(rvar[:, :], rvar[:, :], rstd[:, :], ALU.add).then_inc(S("var_made"), 1)
                v.wait_ge(S("std_made"), n)
                step(v.reciprocal(rstd[:, :], rtmp[:, :]))
                after()
                step(v.tensor_tensor(rtmp[:, :], rstd[:, :], rstd[:, :], ALU.mult))
                after()
                step(v.scalar_tensor_tensor(rtmp[:, :], rtmp[:, :], -0.5, rvar[:, :], ALU.mult, ALU.mult))
                after()
                step(v.scalar_tensor_tensor(rstd[:, :], rtmp[:, :], 1.5, rstd[:, :], ALU.add, ALU.mult))
                after()

            def newton_a(k, name):
                v.tensor_tensor(ra[:, k, :], r0[:, k, :], r0[:, k, :], ALU.mult)
                v.tensor_scalar(rb[:, k, :], ss[:, k, :], -0.5 / D, -0.5 * LN_EPS, ALU.mult, ALU.add)
                v.tensor_scalar(g1[:, k, :], ge[:, k, :], 1.0, None, ALU.add).then_inc(S(name), 1)

            def newton_b(k, name):
                v.tensor_tensor(rc[:, k, :], ra[:, k, :], rb[:, k, :], ALU.mult)
                v.reciprocal(gate[:, k, :], g1[:, k, :]).then_inc(S(name), 1)

            def newton_c(k, name):
                v.scalar_tensor_tensor(r1[:, k, :], rc[:, k, :], 1.5, r0[:, k, :], ALU.add, ALU.mult).then_inc(S(name), 1)

            def scaled(k, name):
                for j in range(J):
                    a = v.scalar_tensor_tensor(msg[:, k, j, 0:D], h[:, k, j, :], r1[:, k, j:j + 1], g_bc[:, :], ALU.mult, ALU.mult)
                a.then_inc(S(name), 1)

            def clipped(k, name):
                v.tensor_tensor(msg[:, k, :, 0:D], msg[:, k, :, 0:D], nb_bc[:, None, :].to_broadcast([P, J, D]), ALU.max).then_inc(S(name), 1)

            def add_rows(to, k, rows, part):
                lo, hi = ((0, 3), (3, J))[part]
                return v.tensor_tensor(h[:, k, lo:hi, :],
                                       to[:, HS[lo]:HS[lo] + (hi - lo) * (D + 1)].rearrange("p (j f) -> p j f", f=D + 1)[:, :, 0:D],
                                       rows[:, lo:hi, :], ALU.add)

            with v.If(general == 0):
                def body(t, base):
                    d, c, e = t.back(4), t.back(3), t.back(7)
                    first = onehot(1, t) if t.within(T) else iter(())
                    next(first, None)
                    if d.within(T):
                        k = d.slot % 2
                        v.wait_ge(S("r0_made"), d.t + 1)
                        newton_a(k, "newton_a")
                    if c.within(T):
                        v.wait_ge(S("h_made"), c.t + 1)
                        v.wait_ge(S("ge_made"), c.t + 1)
                        v.wait_ge(S(f"gathered1_{c.slot}"), (c.lap + 1) * (16 * J))
                        if c.since(2):
                            v.wait_ge(S("scaled"), c.t - 1)
                        add_rows(hp[c.slot % 2], c.slot % 2, Gx[:, c.slot], 0)
                    if d.within(T):
                        v.wait_ge(S("newton_a"), d.t + 1)
                        newton_b(k, "newton_b")
                    if c.within(T):
                        add_rows(hp[c.slot % 2], c.slot % 2, Gx[:, c.slot], 1).then_inc(S("h_added"), 1)
                    if d.within(T):
                        v.wait_ge(S("newton_b"), d.t + 1)
                        newton_c(k, "newton_c")
                        if d.since(2):
                            v.wait_ge(S("sums_made1"), d.t - 1)
                        v.tensor_tensor(Sg[:, k], Ce[:, d.slot, :, ED:C], gate[:, k, :, None].to_broadcast([P, J, W]),
                                        ALU.mult).then_inc(S("Sg_made"), 1)
                    for _ in first:
                        pass
                    if d.within(T):
                        v.wait_ge(S("newton_c"), d.t + 1)
                        scaled(k, "scaled")
                    if e.within(T):
                        add(1, e, base)
                    if d.within(T):
                        v.wait_ge(S("scaled"), d.t + 1)
                        clipped(k, "msg_made")
                turns(v, T, LAG1, body, top=lambda t: bases(v, regs, t.back(7)))
                v.wait_ge(S("added1"), T)
            with v.Else():
                v.memset(fl[:, 0:1], 0.0).then_inc(S("g_summed1"), 1)
                with v.Fori(0, T) as t:
                    v.wait_ge(S("g_h_made"), t + 1)
                    v.wait_ge(S("g_ge_made"), t + 1)
                    v.wait_ge(S("g_gathered1"), (t + 1) * (32 * J))
                    v.wait_ge(S("g_summed1"), t + 1)
                    add_rows(hp[0], 0, Gx[:, 0], 0)
                    add_rows(hp[0], 0, Gx[:, 0], 1).then_inc(S("g_rows"), 1)
                    v.wait_ge(S("g_rows"), t + 1)
                    v.tensor_tensor(h[:, 0], h[:, 0], Gx[:, 1], ALU.add).then_inc(S("g_h_added"), 1)
                    v.wait_ge(S("g_r0_made"), t + 1)
                    newton_a(0, "g_newton_a")
                    v.wait_ge(S("g_newton_a"), t + 1)
                    newton_b(0, "g_newton_b")
                    v.wait_ge(S("g_newton_b"), t + 1)
                    newton_c(0, "g_newton_c")
                    v.wait_ge(S("g_newton_c"), t + 1)
                    scaled(0, "g_scaled")
                    v.wait_ge(S("g_scaled"), t + 1)
                    clipped(0, "g_msg_made")
                    v.wait_ge(S("g_msg_made"), t + 1)
                    add_wide(1, t)
            v.memset(fl[:, 0:1], 0.0).then_inc(S("layer1_summed"), 1)
            v.wait_ge(S("layer1_summed"), 1)

            def body(t, _):
                b = t.back(1)
                if b.within(NC):
                    k = b.slot % 2
                    v.wait_ge(S("gru_mm"), b.t + 1)
                    if b.since(2):
                        v.wait_ge(S("rz_made"), b.t - 1)
                        v.wait_ge(S("n_in"), b.t - 1)
                    v.tensor_tensor(gin[:, k], hp[k][:, :].rearrange("p (a f) -> p a f", a=2),
                                    gb[:, None, :].to_broadcast([P, 2, 4 * D]), ALU.add).then_inc(S("gin_made"), 1)
                c = t.back(2)
                if c.within(NC):
                    k = c.slot % 2
                    v.wait_ge(S("rz_made"), c.t + 1)
                    if c.since(2):
                        v.wait_ge(S("z2_made"), c.t - 1)
                    v.tensor_tensor(nn[:, k], rz[:, k, :, 0:D], gin[:, k, :, 3 * D:4 * D], ALU.mult).then_inc(S("rh"), 1)
                d = t.back(3)
                if d.within(NC):
                    kd = d.slot % 2
                    v.wait_ge(S("n_made"), d.t + 1)
                    v.tensor_tensor(dd[:, kd], nodes[:, blocks(d), :], nn[:, kd], ALU.subtract).then_inc(S("d1"), 1)
                if c.within(NC):
                    v.wait_ge(S("rh"), c.t + 1)
                    v.tensor_tensor(nn[:, k], nn[:, k], gin[:, k, :, 2 * D:3 * D], ALU.add).then_inc(S("n_in"), 1)
                if d.within(NC):
                    v.wait_ge(S("d1"), d.t + 1)
                    v.tensor_tensor(dd[:, kd], dd[:, kd], rz[:, kd, :, D:2 * D], ALU.mult).then_inc(S("d2"), 1)
                    v.tensor_tensor(nn[:, kd], nn[:, kd], nodes[:, blocks(d), :], ALU.add).then_inc(S("d3"), 1)
                    v.wait_ge(S("d3"), d.t + 1)
                    v.tensor_tensor(nodes[:, blocks(d), :], nn[:, kd], dd[:, kd], ALU.add).then_inc(S("z2_made"), 1)
                    rows_stats(d, "z2_made")
            turns(v, NC, 4, body, peel=NPEEL)
            all_rstd(1, "z2_made")

            def body(t, _):
                if t.since(U):
                    v.wait_ge(S(f"stored_{t.slot}"), t.lap * 32)
                for a in range(2):
                    b = bass.ds(t.t * 2 + a, 1)
                    o = v.tensor_scalar(xb[:, t.slot, a:a + 1, :], nodes[:, b, :], mean[:, b], rstd[:, b], ALU.subtract, ALU.mult)
                o.then_inc(S("out_made"), 1)
            turns(v, NC, 0, body, peel=NPEEL)


_INS = ['x', 'src', 'dst', 'edge_attr_64', 'L0_gnn_eps', 'L0_gnn_W1', 'L0_gnn_b1', 'L0_gnn_W2', 'L0_gnn_b2',
        'L1_gnn_W1', 'L1_gnn_b1', 'L1_gnn_ln_g', 'L1_gnn_ln_b', 'L1_gnn_W2', 'L1_gnn_b2', 'L1_gnn_gate_w',
        'L1_gnn_gate_b', 'L1_gnn_W_ih', 'L1_gnn_b_ih', 'L1_gnn_W_hh', 'L1_gnn_b_hh']


def kernel(**inputs):
    import numpy as _np
    import concourse.bacc as _bacc
    from concourse import mybir as _mybir
    from concourse.bass_utils import run_bass_kernel_spmd as _run

    nc = _bacc.Bacc("TRN2", target_bir_lowering=False, num_devices=1)
    arrays, args = {}, []
    for name in _INS:
        a = _np.ascontiguousarray(inputs[name])
        arrays[f"in_{name}_dram"] = a
        args.append(nc.dram_tensor(f"in_{name}_dram", a.shape, _mybir.dt.from_np(a.dtype), kind="ExternalInput").ap())
    o = nc.dram_tensor("out_0_dram", inputs['x'].shape, _mybir.dt.float32, kind="ExternalOutput").ap()
    bass_gnn_kernel(nc, *args, o)
    r = _run(nc, [arrays], core_ids=[0])
    return r.results[0]["out_0_dram"]
```

```python
import concourse.bass as bass
from concourse import mybir
from contextlib import ExitStack

F32 = mybir.dt.float32
I32 = mybir.dt.int32
ALU = mybir.AluOpType
ACT = mybir.ActivationFunctionType
AX = mybir.AxisListType

P = 128
J = 5
G = P * J
W = 32
U = 4
WIDE = 256
LN_EPS = 1e-5




def bass_gnn_kernel(nc, x, src, dst, edge_attr_64, L0_gnn_eps, L0_gnn_W1, L0_gnn_b1, L0_gnn_W2, L0_gnn_b2,
                    L1_gnn_W1, L1_gnn_b1, L1_gnn_ln_g, L1_gnn_ln_b, L1_gnn_W2, L1_gnn_b2, L1_gnn_gate_w,
                    L1_gnn_gate_b, L1_gnn_W_ih, L1_gnn_b_ih, L1_gnn_W_hh, L1_gnn_b_hh, out):
    N, D = x.shape
    E, ED = edge_attr_64.shape
    T = E // G
    R = N * U // T
    NT = -(-N // R)
    NW = -(-N // WIDE)
    NPAD = max(NW * WIDE, NT * R)
    C = ED + W
    M = D + 1
    FR, FG = 125, T // 125
    OFF = 3
    SLACK = 4
    assert D == P and T * G == E and FR * FG == T and R * T == N * U and R <= P and N - 1 + W <= NT * R

    X1D = nc.dram_tensor("x1_rows", [NT * R, D], F32, kind="Internal").ap()
    PD = nc.dram_tensor("P_rows", [NT * R, D], F32, kind="Internal").ap()
    QD = nc.dram_tensor("Q_rows", [NT * R, D], F32, kind="Internal").ap()

    src_v = src.rearrange("(t p j) -> t p j", p=P, j=J)
    dst_v = dst.rearrange("(t p j) -> t p j", p=P, j=J)
    ef_v = edge_attr_64.rearrange("(t p j) d -> t p j d", p=P, j=J)

    with ExitStack() as ctx:
        def sb(name, shape, dt=F32):
            return ctx.enter_context(nc.sbuf_tensor(name, shape, dt))

        def ps(name, shape):
            return ctx.enter_context(nc.psum_tensor(name, shape, F32))

        def sem(name):
            return ctx.enter_context(nc.semaphore(name))

        aggT = sb("aggT", [P, NPAD])
        gsum = sb("gsum", [1, NPAD])
        scratch = sb("scratch", [P, 12000])
        base_bc = sb("base_bc", [P, T])
        base_i = sb("base_i", [1, T + OFF], I32)
        rtmp = sb("rtmp", [1, 4])

        idx = sb("idx", [P, U, J], I32)
        idx2 = sb("idx2", [P, J], I32)
        dsti = sb("dsti", [P, U, J], I32)
        drel = sb("drel", [P, U, J])
        rings = sb("rings", [P, U * J * D + U * J * C])
        Gx = rings[:, 0:U * J * D].rearrange("p (u j d) -> p u j d", u=U, j=J)
        Ce = rings[:, U * J * D:].rearrange("p (u j c) -> p u j c", u=U, j=J)
        CTx = sb("CTx", [P, 2 * J * P])
        CT = CTx[0:C, :].rearrange("c (s e) -> c s e", s=2)
        rhs = sb("rhs", [C, U, D + 1])
        h = sb("h", [P, 2, J, D])
        sq = sb("sq", [P, J, D])
        ss = sb("ss", [P, 2, J])
        lnv = sb("lnv", [P, 2, J])
        r0 = sb("r0", [P, 2, J])
        ra = sb("ra", [P, 2, J])
        rc = sb("rc", [P, 2, J])
        r1 = sb("r1", [P, 2, J])
        ge = sb("ge", [P, 2, J])
        g1 = sb("g1", [P, 2, J])
        gate = sb("gate", [P, 2, J])
        Sg = sb("Sg", [P, 2, J, W])
        msg = sb("msg", [P, 2, J, M])
        Us = sb("Us", [W, M])

        ident = sb("ident", [P, P])
        ones = sb("ones", [P, P])
        iota_i = scratch[:, 11700:11700 + WIDE].bitcast(I32)
        iota = sb("iota", [P, WIDE])
        W1 = sb("W1", [P, D])
        W2 = sb("W2", [P, D])
        b1c = sb("b1c", [P, 1])
        b2bc = sb("b2bc", [P, D])
        eps1 = sb("eps1", [P, 2])
        Wabc = sb("Wabc", [P, 2, D])
        W3g = sb("W3g", [ED, D])
        q_bias = sb("q_bias", [P, 2 * D])
        wmean = sb("wmean", [P, 8])
        g_bc = sb("g_bc", [P, D])
        nb_bc = sb("nb_bc", [P, D])
        lnb_c = sb("lnb_c", [P, 1])
        V2 = sb("V2", [P, D])
        b2row = sb("b2row", [1, 2, D])
        gbias = sb("gbias", [P, 2])
        Wg = scratch[:, 8000:8000 + 6 * D].rearrange("p (a c d) -> p a c d", a=2, c=3)
        WgT = sb("WgT", [P, 2, 3 * D])
        bi = scratch[:, 9000:9000 + 3 * D]
        bh = scratch[:, 10000:10000 + 3 * D]
        b1bc = scratch[:, 6000:6000 + D]
        b_bc = scratch[:, 6200:6200 + D]
        Wab = scratch[:, 6400:6400 + 2 * D].rearrange("p (a d) -> p a d", a=2)
        base_f = scratch[0:1, 7000:7000 + T]
        share_i = scratch[0:1, 11000:11000 + T].bitcast(I32)
        share = scratch[0:1, 3300:3300 + T]
        gb = sb("gb", [P, 4 * D])
        fl = sb("fl", [P, 4])
        fl_i = sb("fl_i", [1, 2], I32)
        epsc = sb("epsc", [P, 1])
        zeros = sb("zeros", [P, R])

        wide = rings[:, 2 * J * D:2 * J * D + J * WIDE].rearrange("p (j w) -> p j w", j=J)
        assert J * WIDE <= 2 * J * D
        h_flat = h[:, :, :, :].rearrange("p s j d -> p (s j d)")
        xa, xr, zt, x1t = (h_flat[0:R, k * D:(k + 1) * D] for k in range(4))
        yT, hT, x1T = (h_flat[:, 4 * D + k * R:4 * D + (k + 1) * R] for k in range(3))
        PQ = h_flat[0:R, 6 * D:8 * D]
        st = h_flat[0:R, 8 * D:8 * D + 16]
        assert 3 * R <= 2 * D
        xa1, xr1, nn, t1, zd, z2t, ot = (scratch[0:R, k * D:(k + 1) * D] for k in range(7))
        rz = scratch[0:R, 7 * D:9 * D]
        xm = scratch[:, 9 * D:9 * D + 2 * R]
        sq1 = scratch[0:R, 11 * D:11 * D + 16]

        hp = [ps(f"hp{i}", [P, 1024]) for i in range(2)]
        cp = ps("cp", [P, 1024])
        up = ps("up", [P, 512])
        vp = ps("vp", [P, 512])
        xm_ps = up[:, 3 * P:3 * P + 2 * R] if 3 * P + 2 * R <= 512 else up[:, 512 - 2 * R:512]
        assert 512 - 2 * R >= M and (J - 4) * P + 2 * D <= 512 and 2 * W + 2 * D <= 512
        rz_ps = cp[0:R, J * P:J * P + 2 * D]
        n_ps = vp[0:R, 2 * W:2 * W + 2 * D]

        s = {}

        def S(name):
            if name not in s:
                s[name] = sem(name)
            return s[name]

        class Step:
            def __init__(self, static, i=None):
                self.static, self.i = static, i

            def back(self, lag):
                return Step(self.static - lag, self.i)

            @property
            def t(self):
                return self.static if self.i is None else self.i * U + self.static

            @property
            def slot(self):
                return self.static % U

            @property
            def lap(self):
                return self.static // U if self.i is None else self.i + self.static // U

            def since(self, first):
                return self.i is not None or self.static >= first

            def within(self, count):
                return self.i is not None or 0 <= self.static < count

        def turns(eng, count, lag, body, top=None, peel=2 * U):
            for k in range(peel):
                body(Step(k), None)
            n = (count - peel) // U
            assert n >= 0
            if n:
                with eng.Fori(0, n) as i:
                    loaded = top(Step(peel, i)) if top else None
                    for k in range(U):
                        body(Step(peel + k, i), loaded[k] if loaded else None)
            for k in range(peel + n * U, count + lag):
                body(Step(k), None)

        def settled(eng):
            eng.sem_inc(S("settled"), 1)

        def flag(eng):
            eng.wait_ge(S("flag_ready"), 1)
            return eng.value_load(fl_i[0:1, 0:1], min_val=0, max_val=1)


        def bases(eng, regs, t):
            eng.load(regs, base_i[0:1, bass.ds(t.t + OFF, U)])
            return [eng.snap(r, min_val=0, max_val=N - 1) for r in regs]

        def one_base(eng, t):
            return eng.value_load(base_i[0:1, t.t + OFF:t.t + OFF + 1], min_val=0, max_val=N - 1)

        class Tile:
            def __init__(self, n, first, last):
                self.n, self.first, self.last = n, first, last

            @property
            def rows(self):
                return N - (NT - 1) * R if self.last else R

        def due(t, lag):
            b = t.back(lag)
            if b.slot or (b.i is None and not 0 <= b.lap < NT):
                return None
            return Tile(b.lap, b.i is None and b.lap == 0, b.i is None and b.lap == NT - 1)

        def tiles(eng, body):
            body(Tile(0, True, False))
            with eng.Fori(1, NT - 1) as n:
                body(Tile(n, False, False))
            body(Tile(NT - 1, False, True))

        def hslots(k):
            return [512 * (j // 3) + (D + 1) * (j % 3) for j in range(J)]

        Y0 = (U - 1) + 4 + SLACK
        Y1 = Y0 + 4
        LAG0, LAG1 = Y0 + 6, Y1 + 10
        PEEL0, PEEL1 = -(-LAG0 // U) * U, -(-LAG1 // U) * U
        HS = hslots(0)
        consts = []

        def row(v):
            return v.rearrange("(a d) -> a d", a=1)

        def col(v):
            return v.rearrange("(d a) -> d a", a=1)

        consts += [
            (W1[:, :], L0_gnn_W1), (W2[:, :], L0_gnn_W2), (b1c[:, :], col(L0_gnn_b1)),
            (b2bc[:, :], row(L0_gnn_b2).to_broadcast([P, D])),
            (eps1[:, 0:1], row(L0_gnn_eps).to_broadcast([P, 1])),
            (Wab[:, 0, :], L1_gnn_W1[0:D, :]), (Wab[:, 1, :], L1_gnn_W1[D:2 * D, :]),
            (W3g[:, :], L1_gnn_W1[2 * D:2 * D + ED, :]),
            (b1bc[:, :], row(L1_gnn_b1).to_broadcast([P, D])),
            (g_bc[:, :], row(L1_gnn_ln_g).to_broadcast([P, D])),
            (b_bc[:, :], row(L1_gnn_ln_b).to_broadcast([P, D])),
            (lnb_c[:, :], col(L1_gnn_ln_b)), (V2[:, :], L1_gnn_W2), (b2row[:, 0, :], row(L1_gnn_b2)),
            (gbias[:, 0:1], row(L1_gnn_gate_b).to_broadcast([P, 1])),
            (Wg[:, 0, :, :], L1_gnn_W_ih.rearrange("(c p) d -> p c d", p=P)),
            (Wg[:, 1, :, :], L1_gnn_W_hh.rearrange("(c p) d -> p c d", p=P)),
            (bi[:, :], row(L1_gnn_b_ih).to_broadcast([P, 3 * D])),
            (bh[:, :], row(L1_gnn_b_hh).to_broadcast([P, 3 * D])),
        ] + [(rhs[0:ED, k, D:D + 1], L1_gnn_gate_w) for k in range(U)]

        block = ctx.enter_context(nc.Block())

        @block.sync
        def _(sp):
            with nc.allow_non_contiguous_dma(reason="small tables"):
                sp.dma_start(aggT[0:FR, 0:FG * G].bitcast(I32),
                             dst.rearrange("(p f) -> p f", p=FR)).then_inc(S("dst_all"), 16)
                sp.dma_start(base_i[0:1, OFF:OFF + T],
                             dst.rearrange("(a t f) -> a t f", a=1, f=G)[:, :, 0]).then_inc(S("base_loaded"), 16)
                for to, frm in consts:
                    sp.dma_start(to, frm).then_inc(S("consts"), 16)
            general = flag(sp)

            def load_group(layer, t):
                if t.since(U):
                    sp.wait_ge(S(f"gathered{layer}_{t.slot}"), t.lap * (16 * J))
                sp.dma_start(idx[:, t.slot, :], src_v[t.t, :, :]).then_inc(S(f"idx{layer}_{t.slot}"), 16)
                if t.since(U):
                    sp.wait_ge(S(f"onehot{layer}"), t.t - (U - 1))
                sp.dma_start(dsti[:, t.slot, :], dst_v[t.t, :, :]).then_inc(S(f"dst{layer}_{t.slot}"), 16)

            def load_x(q, to, name, used):
                if not q.first:
                    sp.wait_ge(S(used), q.n)
                sp.dma_start(to[0:q.rows, :], x[bass.ds(q.n * R, q.rows), :]).then_inc(S(name), 16)

            def store_x1(q):
                sp.wait_ge(S("x1_made"), q.n + 1)
                sp.dma_start(X1D[bass.ds(q.n * R, R), :], x1t).then_inc(S("x1_stored"), 16)

            def store_pq(q):
                sp.wait_ge(S("pq_made"), q.n + 1)
                for a, to in enumerate((PD, QD)):
                    sp.dma_start(to[bass.ds(q.n * R, R), :], PQ[:, a * D:(a + 1) * D]).then_inc(S("pq_stored"), 16)

            with sp.If(general == 0):
                def body(t, base):
                    if t.within(T):
                        load_group(0, t)
                    if due(t, Y0 - 2):
                        load_x(due(t, Y0 - 2), xa, "xa_loaded", "x_turned")
                    if due(t, Y0):
                        load_x(due(t, Y0), xr, "xr_loaded", "z_made")
                    if due(t, Y0 + 4):
                        store_x1(due(t, Y0 + 4))
                    if due(t, Y0 + 6):
                        store_pq(due(t, Y0 + 6))
                turns(sp, T, LAG0, body, peel=PEEL0)
            with sp.Else():
                with sp.Fori(0, T) as t:
                    sp.wait_ge(S("g_summed0"), t + 1)
                    sp.dma_start(idx[:, 0, :], src_v[t, :, :]).then_inc(S("g_idx0"), 16)
                    sp.dma_start(dsti[:, 0, :], dst_v[t, :, :]).then_inc(S("g_idx0"), 16)

                def body(q):
                    load_x(q, xa, "xa_loaded", "x_turned")
                    load_x(q, xr, "xr_loaded", "z_made")
                    store_x1(q)
                    store_pq(q)
                tiles(sp, body)
            sp.wait_ge(S("x1_stored"), 16 * NT)
            sp.wait_ge(S("pq_stored"), 32 * NT)

            def load_x1(q, to, name, used):
                if not q.first:
                    sp.wait_ge(S(used), q.n)
                sp.dma_start(to, X1D[bass.ds(q.n * R, R), :]).then_inc(S(name), 16)

            def store_out(q):
                sp.wait_ge(S("out_made"), q.n + 1)
                sp.dma_start(out[bass.ds(q.n * R, q.rows), :], ot[0:q.rows, :]).then_inc(S("out_stored"), 16)

            with sp.If(general == 0):
                def body(t, base):
                    if t.within(T):
                        load_group(1, t)
                        if t.since(U):
                            sp.wait_ge(S("tile_turned"), t.t - (U - 1))
                        sp.dma_start(Ce[:, t.slot, :, 0:ED], ef_v[t.t, :, :, :]).then_inc(S(f"ef_{t.slot}"), 16)
                        if t.since(U):
                            sp.wait_ge(S("h_made"), t.t - (U - 1))
                        if base is None:
                            base = one_base(sp, t)
                        sp.dma_start(rhs[ED:C, t.slot, 0:D], QD[bass.ds(base, W), :]).then_inc(S(f"win_{t.slot}"), 16)
                    if due(t, Y1 - 2):
                        load_x1(due(t, Y1 - 2), xa1, "xa1_loaded", "xm_mm")
                    if due(t, Y1 + 4):
                        load_x1(due(t, Y1 + 4), xr1, "xr1_loaded", "z2_made")
                    if due(t, Y1 + 10):
                        store_out(due(t, Y1 + 10))
                regs = [sp.alloc_register(f"sp_base{k}") for k in range(U)]
                turns(sp, T, LAG1, body, top=lambda t: bases(sp, regs, t), peel=PEEL1)
            with sp.Else():
                with sp.Fori(0, T) as t:
                    sp.wait_ge(S("g_summed1"), t + 1)
                    sp.dma_start(idx[:, 0, :], src_v[t, :, :]).then_inc(S("g_idx1"), 16)
                    sp.dma_start(dsti[:, 0, :], dst_v[t, :, :]).then_inc(S("g_idx1"), 16)
                    sp.dma_start(idx2[:, :], dst_v[t, :, :]).then_inc(S("g_idx1"), 16)
                    sp.dma_start(Ce[:, 3, :, 0:ED], ef_v[t, :, :, :]).then_inc(S("g_idx1"), 16)

                def body(q):
                    load_x1(q, xa1, "xa1_loaded", "xm_mm")
                    load_x1(q, xr1, "xr1_loaded", "z2_made")
                    store_out(q)
                tiles(sp, body)
            sp.wait_ge(S("out_stored"), 16 * NT)

        @block.gpsimd
        def _(pool):
            pool.iota(iota_i[:, :], pattern=[[1, WIDE]], base=0, channel_multiplier=0).then_inc(S("iota_made"), 1)
            pool.iota(share_i[:, :], pattern=[[R // U, T]], base=0, channel_multiplier=0).then_inc(S("iota_made"), 1)
            pool.memset(ones[:, :], 1.0).then_inc(S("ones_made"), 1)
            pool.wait_ge(S("ones_made"), 1)
            pool.affine_select(out=ident[:, :], in_=ones[:, :], compare_op=ALU.is_equal, fill=0.0, base=0,
                               pattern=[[1, P]], channel_multiplier=-1).then_inc(S("ident_made"), 1)
            general = flag(pool)

            def gather(to, table, index, name):
                settled(pool)
                for j in range(J):
                    pool.indirect_dma_start(to[:, j, :], None, table,
                                            bass.IndirectOffsetOnAxis(ap=index[:, j:j + 1], axis=0)).then_inc(S(name), 16)

            for layer, table in ((0, x), (1, PD)):
                if layer:
                    pool.wait_ge(S("pq_stored"), 32 * NT)
                with pool.If(general == 0):
                    def body(t, _):
                        pool.wait_ge(S(f"idx{layer}_{t.slot}"), (t.lap + 1) * 16)
                        if t.since(U):
                            pool.wait_ge(S("h_added" if layer else "sums_made0"), t.t - (U - 1))
                        gather(Gx[:, t.slot], table, idx[:, t.slot], f"gathered{layer}_{t.slot}")
                    turns(pool, T, 0, body)
                with pool.Else():
                    with pool.Fori(0, T) as t:
                        pool.wait_ge(S(f"g_idx{layer}"), (t + 1) * (64 if layer else 32))
                        gather(Gx[:, 0], table, idx[:, 0], f"g_gathered{layer}")
                        if layer:
                            gather(Gx[:, 1], QD, idx2, f"g_gathered{layer}")

        @block.tensor
        def _(pe):
            pe.wait_ge(S("ident_made"), 1)
            pe.wait_ge(S("range_rows"), 1)
            pe.matmul(up[0:1, 0:FR], fl[0:FR, 2:3], ident[0:FR, 0:FR], start=True, stop=True).then_inc(S("range_row"), 1)
            pe.wait_ge(S("base_float"), 1)
            for a in range(0, T, 512):
                n = min(512, T - a)
                mm = pe.matmul(cp[:, a:a + n], ones[0:1, :], base_f[0:1, a:a + n], start=True, stop=True)
            mm.then_inc(S("base_spread"), 1)
            pe.wait_ge(S("consts"), 16 * len(consts))
            for a in range(2):
                for k in range(3):
                    mm = pe.transpose(hp[a][:, k * P:(k + 1) * P], Wg[:, a, k, :], ident[:, :])
            mm.then_inc(S("gru_turned"), 1)
            pe.matmul(hp[0][0:1, 512:512 + D], lnb_c[:, :], V2[:, :], start=True, stop=True).then_inc(S("b2_made"), 1)
            general = flag(pe)

            def window_sums(layer, t):
                pe.wait_ge(S("msg_made" if layer else "onehot0"), t.t + 1)
                if not layer:
                    pe.wait_ge(S(f"gathered0_{t.slot}"), (t.lap + 1) * (16 * J))
                if t.since(1):
                    pe.wait_ge(S(f"sums_copied{layer}"), t.t)
                for j in range(J):
                    if layer:
                        mm = pe.matmul(up[0:W, 0:M], Sg[:, t.slot % 2, j, :], msg[:, t.slot % 2, j, :],
                                       start=(j == 0), stop=(j == J - 1))
                    else:
                        mm = pe.matmul(up[0:W, 0:D], Ce[:, t.slot, j, ED:C], Gx[:, t.slot, j, :],
                                       start=(j == 0), stop=(j == J - 1))
                mm.then_inc(S(f"sums_made{layer}"), 1)

            def turn_sums(layer, t):
                pe.wait_ge(S(f"sums_copied{layer}"), t.t + 1)
                if t.since(1):
                    pe.wait_ge(S(f"added{layer}"), t.t)
                settled(pe)
                mm = pe.transpose(vp[:, 0:W], Us[:, 0:D], ident[0:W, 0:W])
                if layer:
                    mm = pe.transpose(vp[0:1, W:2 * W], Us[:, D:M], ident[0:W, 0:W])
                mm.then_inc(S(f"sums_turned{layer}"), 1)

            def turn_x(q):
                pe.wait_ge(S("xa_loaded"), (q.n + 1) * 16)
                if not q.first:
                    pe.wait_ge(S("y_made"), q.n)
                settled(pe)
                pe.transpose(cp[:, 0:R], xa, ident[0:R, 0:R]).then_inc(S("x_turned"), 1)

            def hidden(q):
                pe.wait_ge(S("y_made"), q.n + 1)
                if not q.first:
                    pe.wait_ge(S("hidden_made"), q.n)
                settled(pe)
                pe.matmul(cp[:, 512:512 + R], W1[:, :], yT, start=True, stop=True).then_inc(S("hidden_mm"), 1)

            def mlp(q):
                pe.wait_ge(S("hidden_made"), q.n + 1)
                if not q.first:
                    pe.wait_ge(S("z_made"), q.n)
                settled(pe)
                pe.matmul(hp[0][0:R, 0:D], hT, W2[:, :], start=True, stop=True).then_inc(S("mlp_mm"), 1)

            def turn_x1(q):
                pe.wait_ge(S("x1_made"), q.n + 1)
                if not q.first:
                    pe.wait_ge(S("x1T_copied"), q.n)
                settled(pe)
                pe.transpose(hp[0][:, 512:512 + R], x1t, ident[0:R, 0:R]).then_inc(S("x1_turned"), 1)

            def pq(q):
                pe.wait_ge(S("x1T_copied"), q.n + 1)
                if not q.first:
                    pe.wait_ge(S("pq_made"), q.n)
                settled(pe)
                pe.matmul(hp[1][0:R, 0:2 * D], x1T, Wabc[:, :, :], start=True, stop=True).then_inc(S("pq_mm"), 1)

            pe.wait_ge(S("base_saved"), 1)
            with pe.If(general == 0):
                def body(t, _):
                    if t.back(2).within(T):
                        window_sums(0, t.back(2))
                    if t.back(3).within(T):
                        turn_sums(0, t.back(3))
                    if due(t, Y0 - 1):
                        turn_x(due(t, Y0 - 1))
                    if due(t, Y0):
                        hidden(due(t, Y0))
                    if due(t, Y0 + 1):
                        mlp(due(t, Y0 + 1))
                    if due(t, Y0 + 3):
                        turn_x1(due(t, Y0 + 3))
                    if due(t, Y0 + 4):
                        pq(due(t, Y0 + 4))
                turns(pe, T, LAG0, body, peel=PEEL0)
            with pe.Else():
                with pe.Fori(0, T) as t:
                    with pe.Fori(0, NW) as w:
                        pe.wait_ge(S("g_gathered0"), (t + 1) * (16 * J))
                        pe.wait_ge(S("g_wide0"), t * NW + w + 1)
                        for j in range(J):
                            mm = pe.matmul(cp[:, 0:WIDE], Gx[:, 0, j, :], wide[:, j, :], start=(j == 0), stop=(j == J - 1))
                        mm.then_inc(S("g_sums0"), 1)

                pe.wait_ge(S("g_summed0"), T + 1)

                def body(q):
                    turn_x(q)
                    hidden(q)
                    mlp(q)
                    turn_x1(q)
                    pq(q)
                tiles(pe, body)
            pe.wait_ge(S("pq_made"), NT)

            def mix(q):
                pe.wait_ge(S("xa1_loaded"), (q.n + 1) * 16)
                if not q.first:
                    pe.wait_ge(S("xm_copied"), q.n)
                settled(pe)
                pe.transpose(xm_ps[:, 0:R], xa1, ident[0:R, 0:R])
                at = bass.ds(q.n * R, R)
                pe.matmul(xm_ps[:, R:2 * R], V2[:, :], aggT[:, at], start=True, stop=False)
                pe.matmul(xm_ps[:, R:2 * R], b2row[0:1, 1, :], gsum[0:1, at], start=False, stop=True).then_inc(S("xm_mm"), 1)

            def gru_rz(q):
                pe.wait_ge(S("xm_copied"), q.n + 1)
                if not q.first:
                    pe.wait_ge(S("rz_clamped"), q.n)
                settled(pe)
                pe.matmul(rz_ps, ones[0:1, 0:R], gb[0:1, 0:2 * D], start=True, stop=False)
                pe.matmul(rz_ps, xm[:, R:2 * R], WgT[:, 0, 0:2 * D], start=False, stop=False)
                pe.matmul(rz_ps, xm[:, 0:R], WgT[:, 1, 0:2 * D], start=False, stop=True).then_inc(S("rz_mm"), 1)

            def gru_n(q):
                pe.wait_ge(S("xm_copied"), q.n + 1)
                if not q.first:
                    pe.wait_ge(S("n_in"), q.n)
                settled(pe)
                for k, a in ((0, R), (1, 0)):
                    to = n_ps[:, k * D:(k + 1) * D]
                    pe.matmul(to, ones[0:1, 0:R], gb[0:1, (2 + k) * D:(3 + k) * D], start=True, stop=False)
                    mm = pe.matmul(to, xm[:, a:a + R], WgT[:, k, 2 * D:3 * D], start=False, stop=True)
                mm.then_inc(S("n_mm"), 1)

            with pe.If(general == 0):
                def body(t, _):
                    b, c = t.back(1), t.back(2)
                    if due(t, Y1 + 2):
                        if b.within(T + 1):
                            pe.wait_ge(S("tile_copied"), b.t)
                        gru_rz(due(t, Y1 + 2))
                    if b.within(T):
                        pe.wait_ge(S("onehot1"), b.t + 1)
                        pe.wait_ge(S(f"ef_{b.slot}"), (b.lap + 1) * 16)
                        if b.since(1):
                            pe.wait_ge(S("tile_copied"), b.t)
                        if due(t, Y1 + 3):
                            pe.wait_ge(S("rz_clamped"), due(t, Y1 + 3).n + 1)
                        for j in range(J):
                            mm = pe.transpose(cp[0:C, j * P:(j + 1) * P], Ce[:, b.slot, j, :], ident[:, :])
                        mm.then_inc(S("tile_turned"), 1)
                    if c.within(T):
                        pe.wait_ge(S("tile_copied"), c.t + 1)
                        pe.wait_ge(S(f"win_{c.slot}"), (c.lap + 1) * 16)
                        if c.since(2):
                            pe.wait_ge(S("h_added"), c.t - 1)
                            pe.wait_ge(S("ge_made"), c.t - 1)
                        for j in range(J):
                            mm = pe.matmul(hp[c.slot % 2][:, HS[j]:HS[j] + D + 1], CT[:, c.slot % 2, j * P:(j + 1) * P],
                                           rhs[:, c.slot, :], start=True, stop=True)
                        mm.then_inc(S("h_made"), 1)
                    if due(t, Y1 + 1):
                        pe.wait_ge(S("xm_copied"), due(t, Y1 + 1).n + 1)
                    if due(t, Y1):
                        pe.wait_ge(S("added1"), t.t - 7 if t.i is not None else min(t.static - 7, T))
                        if t.back(6).within(T):
                            pe.wait_ge(S("sums_copied1"), t.back(6).t + 1)
                        mix(due(t, Y1))
                    if t.back(5).within(T):
                        window_sums(1, t.back(5))
                    if due(t, Y1 + 4):
                        pe.wait_ge(S("n_in"), due(t, Y1 + 4).n + 1)
                    if t.back(6).within(T):
                        turn_sums(1, t.back(6))
                    if due(t, Y1 + 3):
                        if t.back(7).within(T):
                            pe.wait_ge(S("added1"), t.back(7).t + 1)
                        gru_n(due(t, Y1 + 3))
                turns(pe, T, LAG1, body, peel=PEEL1)
            with pe.Else():
                with pe.Fori(0, T) as t:
                    pe.wait_ge(S("g_idx1"), (t + 1) * 64)
                    settled(pe)
                    for j in range(J):
                        mm = pe.transpose(cp[0:ED, j * P:(j + 1) * P], Ce[:, 3, j, 0:ED], ident[:, :])
                    mm.then_inc(S("tile_turned"), 1)
                    pe.wait_ge(S("tile_copied"), t + 1)
                    for j in range(J):
                        mm = pe.matmul(hp[0][:, HS[j]:HS[j] + D + 1], CT[0:ED, 0, j * P:(j + 1) * P],
                                       rhs[0:ED, 0, :], start=True, stop=True)
                    mm.then_inc(S("h_made"), 1)
                    with pe.Fori(0, NW) as w:
                        pe.wait_ge(S("g_wide1"), t * NW + w + 1)
                        for j in range(J):
                            pe.matmul(cp[:, 0:WIDE], msg[:, 0, j, 0:D], wide[:, j, :], start=(j == 0), stop=(j == J - 1))
                        for j in range(J):
                            mm = pe.matmul(cp[0:1, 512:512 + WIDE], msg[:, 0, j, D:M], wide[:, j, :], start=(j == 0), stop=(j == J - 1))
                        mm.then_inc(S("g_sums1"), 1)

                pe.wait_ge(S("g_summed1"), T + 1)

                def body(q):
                    mix(q)
                    gru_rz(q)
                    gru_n(q)
                tiles(pe, body)

        @block.scalar
        def _(act):
            general = flag(act)

            def copy_sums(layer, t):
                act.wait_ge(S(f"sums_made{layer}"), t.t + 1)
                if t.since(1):
                    act.wait_ge(S(f"sums_turned{layer}"), t.t)
                n = M if layer else D
                act.activation(Us[:, 0:n], up[0:W, 0:n], ACT.Copy).then_inc(S(f"sums_copied{layer}"), 1)

            def relu(q):
                act.wait_ge(S("hidden_mm"), q.n + 1)
                if not q.first:
                    act.wait_ge(S("mlp_mm"), q.n)
                act.activation(hT, cp[:, 512:512 + R], ACT.Relu, bias=b1c[:, 0:1]).then_inc(S("hidden_made"), 1)

            def root(q):
                act.wait_ge(S("var_z"), q.n + 1)
                act.activation(st[:, 9:10], st[:, 8:9], ACT.Sqrt).then_inc(S("std_z"), 1)

            def copy_x1T(q):
                act.wait_ge(S("x1_turned"), q.n + 1)
                if not q.first:
                    act.wait_ge(S("pq_mm"), q.n)
                act.activation(x1T, hp[0][:, 512:512 + R], ACT.Copy).then_inc(S("x1T_copied"), 1)

            with act.If(general == 0):
                def body(t, _):
                    if t.back(2).within(T):
                        copy_sums(0, t.back(2))
                    if due(t, Y0 + 1):
                        relu(due(t, Y0 + 1))
                    if due(t, Y0 + 2):
                        root(due(t, Y0 + 2))
                    if due(t, Y0 + 4):
                        copy_x1T(due(t, Y0 + 4))
                turns(act, T, LAG0, body, peel=PEEL0)
            with act.Else():
                def body(q):
                    relu(q)
                    root(q)
                    copy_x1T(q)
                tiles(act, body)

            def gate_exp(k, name):
                for lo, hi in ((0, 3), (3, J)):
                    a = act.activation(ge[:, k, lo:hi].unsqueeze(2),
                                       hp[k][:, HS[lo]:HS[lo] + (hi - lo) * (D + 1)].rearrange("p (j f) -> p j f", f=D + 1)[:, :, D:D + 1],
                                       ACT.Exp, scale=-1.0, bias=gbias[:, 1:2])
                a.then_inc(S(name), 1)

            def squares(k, name):
                for j in range(J):
                    a = act.activation(sq[:, j, :], h[:, k, j, :], ACT.Square, accum_out=ss[:, k, j:j + 1])
                a.then_inc(S(name), 1)

            def guess(k, logs, name, n):
                act.activation(lnv[:, k, :], ss[:, k, :], ACT.Ln, scale=1.0 / D, bias=epsc[:, 0:1]).then_inc(S(logs), 1)
                act.wait_ge(S(logs), n)
                act.activation(r0[:, k, :], lnv[:, k, :], ACT.Exp, scale=-0.5).then_inc(S(name), 1)

            def copy_xm(q):
                act.wait_ge(S("xm_mm"), q.n + 1)
                if not q.first:
                    act.wait_ge(S("rz_mm"), q.n)
                    act.wait_ge(S("n_mm"), q.n)
                act.activation(xm, xm_ps, ACT.Copy).then_inc(S("xm_copied"), 1)

            def inverse(rows, q, exps, logs, name):
                act.wait_ge(S(exps), q.n + 1)
                act.activation(rows, rows, ACT.Ln, bias=ones[0:R, 0:1]).then_inc(S(logs), 1)
                yield
                act.wait_ge(S(logs), q.n + 1)
                act.activation(rows, rows, ACT.Exp, scale=-1.0).then_inc(S(name), 1)

            def rz_exp(q):
                act.wait_ge(S("rz_clamped"), q.n + 1)
                act.activation(rz, rz, ACT.Exp, scale=-1.0).then_inc(S("rz_exp"), 1)
                yield
                yield from inverse(rz, q, "rz_exp", "rz_log", "rz_made")

            def n_exp(q):
                act.wait_ge(S("n_clamped"), q.n + 1)
                act.activation(nn, nn, ACT.Exp, scale=2.0).then_inc(S("n_exp"), 1)
                yield
                yield from inverse(nn, q, "n_exp", "n_log", "n_made")

            def guess_out(q):
                act.wait_ge(S("var_z2"), q.n + 1)
                act.activation(sq1[:, 9:10], sq1[:, 8:9], ACT.Ln).then_inc(S("z2_log"), 1)
                yield
                act.wait_ge(S("z2_log"), q.n + 1)
                act.activation(sq1[:, 10:11], sq1[:, 9:10], ACT.Exp, scale=-0.5).then_inc(S("z2_guess"), 1)

            act.preload_act_table_set("natural_log_exp_and_others")
            with act.If(general == 0):
                def body(t, _):
                    b, c = t.back(1), t.back(3)
                    if c.within(T):
                        act.wait_ge(S("h_made"), c.t + 1)
                        if c.since(2):
                            act.wait_ge(S("msg_made"), c.t - 1)
                        gate_exp(c.slot % 2, "ge_made")
                    if t.back(6).within(T):
                        copy_sums(1, t.back(6))
                    if due(t, Y1 + 1):
                        if t.back(6).within(T):
                            act.wait_ge(S("sums_made1"), t.back(6).t + 1)
                        copy_xm(due(t, Y1 + 1))
                    if b.within(T):
                        act.wait_ge(S("tile_turned"), b.t + 1)
                        if b.since(2):
                            act.wait_ge(S("h_made"), b.t - 1)
                        act.activation(CT[:, b.slot % 2, :], cp[0:C, 0:J * P], ACT.Copy).then_inc(S("tile_copied"), 1)
                    part = iter(())
                    if due(t, Y1 + 3):
                        part = rz_exp(due(t, Y1 + 3))
                    if due(t, Y1 + 5):
                        part = n_exp(due(t, Y1 + 5))
                    if due(t, Y1 + 8):
                        part = guess_out(due(t, Y1 + 8))
                    next(part, None)
                    if c.within(T):
                        act.wait_ge(S("h_added"), c.t + 1)
                        if c.since(1):
                            act.wait_ge(S("squares"), c.t)
                        squares(c.slot % 2, "squares")
                    next(part, None)
                    if c.within(T):
                        act.wait_ge(S("squares"), c.t + 1)
                        guess(c.slot % 2, "logs", "r0_made", c.t + 1)
                    for _ in part:
                        pass
                turns(act, T, LAG1, body, peel=PEEL1)
            with act.Else():
                with act.Fori(0, T) as t:
                    act.wait_ge(S("tile_turned"), t + 1)
                    act.activation(CT[0:ED, 0, :], cp[0:ED, 0:J * P], ACT.Copy).then_inc(S("tile_copied"), 1)
                    act.wait_ge(S("h_made"), t + 1)
                    gate_exp(0, "ge_made")
                    act.wait_ge(S("h_added"), t + 1)
                    squares(0, "squares")
                    act.wait_ge(S("squares"), t + 1)
                    guess(0, "logs", "r0_made", t + 1)


                def body(q):
                    copy_xm(q)
                    for part in (rz_exp, n_exp, guess_out):
                        for _ in part(q):
                            pass
                tiles(act, body)

        @block.vector
        def _(v):
            v.wait_ge(S("dst_all"), 16)
            allv = aggT[0:FR, 0:FG * G].bitcast(I32).rearrange("p (g f) -> p g f", f=G)
            relv = scratch[0:FR, 0:FG * G].rearrange("p (g f) -> p g f", f=G)
            v.tensor_tensor(relv, allv, allv[:, :, 0:1].to_broadcast([FR, FG, G]), ALU.subtract).then_inc(S("rel"), 1)
            v.wait_ge(S("rel"), 1)
            v.tensor_reduce(fl[0:FR, 0:1], relv, AX.XY, ALU.max)
            v.tensor_reduce(fl[0:FR, 1:2], relv, AX.XY, ALU.min).then_inc(S("rel"), 1)
            v.wait_ge(S("rel"), 2)
            v.tensor_scalar(fl[0:FR, 3:4], fl[0:FR, 0:1], float(-(W - 1)), None, ALU.add).then_inc(S("rel"), 1)
            v.wait_ge(S("rel"), 3)
            v.scalar_tensor_tensor(fl[0:FR, 2:3], fl[0:FR, 1:2], -1.0, fl[0:FR, 3:4], ALU.mult, ALU.max).then_inc(S("range_rows"), 1)
            v.wait_ge(S("base_loaded"), 16)
            v.tensor_copy(base_f[:, :], base_i[0:1, OFF:OFF + T]).then_inc(S("base_float"), 1)
            v.wait_ge(S("range_row"), 1)
            v.wait_ge(S("iota_made"), 2)
            v.tensor_copy(share[:, :], share_i[:, :]).then_inc(S("rel"), 1)
            v.wait_ge(S("rel"), 4)
            v.wait_ge(S("base_float"), 1)
            v.tensor_tensor(share[:, :], share[:, :], base_f[:, :], ALU.subtract)
            v.tensor_reduce(rtmp[0:1, 0:1], up[0:1, 0:FR], AX.X, ALU.max).then_inc(S("rel"), 1)
            v.wait_ge(S("rel"), 5)
            v.tensor_reduce(rtmp[0:1, 1:2], share[:, :], AX.X, ALU.max).then_inc(S("rel"), 1)
            v.wait_ge(S("rel"), 6)
            v.scalar_tensor_tensor(rtmp[0:1, 2:3], rtmp[0:1, 1:2], float(-SLACK * (R // U)), rtmp[0:1, 0:1], ALU.add, ALU.max).then_inc(S("rel"), 1)
            v.wait_ge(S("rel"), 7)
            v.tensor_scalar(fl_i[0:1, 0:1], rtmp[0:1, 2:3], 0.0, None, ALU.is_gt).then_inc(S("flag_ready"), 1)
            v.wait_ge(S("base_spread"), 1)
            v.tensor_copy(base_bc[:, :], cp[:, 0:T])
            v.wait_ge(S("iota_made"), 1)
            v.tensor_copy(iota[:, :], iota_i[:, :])
            v.memset(aggT[:, :], 0.0)
            v.memset(gsum[:, :], 0.0).then_inc(S("base_saved"), 1)
            v.wait_ge(S("base_saved"), 1)
            general = flag(v)

            v.wait_ge(S("consts"), 16 * len(consts))
            steps = [0]

            def step(ins):
                steps[0] += 1
                ins.then_inc(S("tables"), 1)

            def after():
                v.wait_ge(S("tables"), steps[0])
            v.tensor_scalar(eps1[:, 1:2], eps1[:, 0:1], 1.0, None, ALU.add)
            v.memset(epsc[:, :], LN_EPS)
            v.memset(zeros[:, :], 0.0)
            v.memset(msg[:, :, :, D:M], 1.0)
            v.memset(q_bias[:, 0:D], 0.0)
            for k in range(U):
                v.memset(rhs[ED:C, k, D:D + 1], 0.0)
            v.tensor_scalar(gbias[:, 1:2], gbias[:, 0:1], -1.0, None, ALU.mult)
            v.tensor_scalar(g_bc[:, :], g_bc[:, :], -0.5 / D, None, ALU.mult)
            v.tensor_scalar(nb_bc[:, :], b_bc[:, :], -1.0, None, ALU.mult)
            v.tensor_tensor(gb[:, 0:2 * D], bi[:, 0:2 * D], bh[:, 0:2 * D], ALU.add)
            v.tensor_copy(gb[:, 2 * D:3 * D], bi[:, 2 * D:3 * D])
            v.tensor_copy(gb[:, 3 * D:4 * D], bh[:, 2 * D:3 * D])
            v.wait_ge(S("gru_turned"), 1)
            for a in range(2):
                v.tensor_copy(WgT[:, a, :], hp[a][:, 0:3 * D])
            v.wait_ge(S("b2_made"), 1)
            v.tensor_tensor(b2row[0:1, 1, :], b2row[0:1, 0, :], hp[0][0:1, 512:512 + D], ALU.add)
            v.tensor_reduce(wmean[:, 0:2], Wab[:, :, :], AX.X, ALU.add)
            v.tensor_reduce(wmean[0:ED, 2:3], W3g[:, :], AX.X, ALU.add)
            step(v.tensor_reduce(wmean[:, 3:4], b1bc[:, :], AX.X, ALU.add))
            after()
            step(v.tensor_scalar(wmean[:, 4:6], wmean[:, 0:2], -1.0 / D, None, ALU.mult))
            step(v.tensor_scalar(wmean[0:ED, 6:7], wmean[0:ED, 2:3], -1.0 / D, None, ALU.mult))
            step(v.tensor_scalar(wmean[:, 7:8], wmean[:, 3:4], -1.0 / D, None, ALU.mult))
            after()
            for a in range(2):
                v.tensor_scalar(Wabc[:, a, :], Wab[:, a, :], wmean[:, 4 + a:5 + a], None, ALU.add)
            for k in range(U):
                v.tensor_scalar(rhs[0:ED, k, 0:D], W3g[:, :], wmean[0:ED, 6:7], None, ALU.add)
            step(v.tensor_scalar(q_bias[:, D:2 * D], b1bc[:, :], wmean[:, 7:8], None, ALU.add))
            after()

            def onehot(layer, t):
                v.wait_ge(S(f"dst{layer}_{t.slot}"), (t.lap + 1) * 16)
                v.tensor_scalar(drel[:, t.slot, :], dsti[:, t.slot, :], base_bc[:, t.t:t.t + 1] if t.i is None else base_bc[:, bass.ds(t.t, 1)],
                                None, ALU.subtract).then_inc(S(f"drel{layer}"), 1)
                if layer:
                    yield
                v.wait_ge(S(f"drel{layer}"), t.t + 1)
                if t.since(U):
                    v.wait_ge(S("tile_turned" if layer else "sums_made0"), t.t - (U - 1))
                if layer and t.since(U):
                    v.wait_ge(S("Sg_made"), t.t - (U - 1))
                v.tensor_tensor(Ce[:, t.slot, :, ED:C], iota[:, None, 0:W].to_broadcast([P, J, W]),
                                drel[:, t.slot, :, None].to_broadcast([P, J, W]), ALU.is_equal).then_inc(S(f"onehot{layer}"), 1)

            def add(layer, t, base):
                if base is None:
                    base = one_base(v, t)
                v.wait_ge(S(f"sums_turned{layer}"), t.t + 1)
                if t.since(1):
                    v.wait_ge(S(f"added{layer}"), t.t)
                a = v.tensor_tensor(aggT[:, bass.ds(base, W)], aggT[:, bass.ds(base, W)], vp[:, 0:W], ALU.add)
                if layer:
                    a = v.tensor_tensor(gsum[0:1, bass.ds(base, W)], gsum[0:1, bass.ds(base, W)], vp[0:1, W:2 * W], ALU.add)
                a.then_inc(S(f"added{layer}"), 1)

            def add_wide(layer, t):
                v.tensor_copy(drel[:, 0, :], dsti[:, 0, :]).then_inc(S(f"g_drel{layer}"), 1)
                with v.Fori(0, NW) as w:
                    v.wait_ge(S(f"g_drel{layer}"), t * (NW + 1) + w + 1)
                    for j in range(J):
                        if layer:
                            a = v.tensor_scalar(wide[:, j, :], iota[:, :], drel[:, 0, j:j + 1], gate[:, 0, j:j + 1], ALU.is_equal, ALU.mult)
                        else:
                            a = v.tensor_scalar(wide[:, j, :], iota[:, :], drel[:, 0, j:j + 1], None, ALU.is_equal)
                    a.then_inc(S(f"g_wide{layer}"), 1)
                    v.wait_ge(S(f"g_wide{layer}"), t * NW + w + 1)
                    v.tensor_scalar(drel[:, 0, :], drel[:, 0, :], float(-WIDE), None, ALU.add).then_inc(S(f"g_drel{layer}"), 1)
                    v.wait_ge(S(f"g_sums{layer}"), t * NW + w + 1)
                    to = bass.ds(w * WIDE, WIDE)
                    a = v.tensor_tensor(aggT[:, to], aggT[:, to], cp[:, 0:WIDE], ALU.add)
                    if layer:
                        a = v.tensor_tensor(gsum[0:1, to], gsum[0:1, to], cp[0:1, 512:512 + WIDE], ALU.add)
                    a.then_inc(S(f"g_added{layer}"), 1)
                v.wait_ge(S(f"g_added{layer}"), t * NW + NW)
                v.memset(fl[:, 0:1], 0.0).then_inc(S(f"g_summed{layer}"), 1)

            def y(q):
                at = bass.ds(q.n * R, R)
                v.wait_ge(S("x_turned"), q.n + 1)
                if not q.first:
                    v.wait_ge(S("hidden_mm"), q.n)
                v.scalar_tensor_tensor(yT, cp[:, 0:R], eps1[:, 1:2], aggT[:, at], ALU.mult, ALU.add).then_inc(S("y_made"), 1)
                v.wait_ge(S("y_made"), q.n + 1)
                v.tensor_tensor(aggT[:, at], zeros[:, :], zeros[:, :], ALU.add).then_inc(S("sums_cleared"), 1)

            def z(q):
                v.wait_ge(S("mlp_mm"), q.n + 1)
                v.wait_ge(S("xr_loaded"), (q.n + 1) * 16)
                v.tensor_tensor(zt, hp[0][0:R, 0:D], xr, ALU.add).then_inc(S("z_made"), 1)
                v.wait_ge(S("z_made"), q.n + 1)
                v.tensor_tensor(zt, zt, b2bc[0:R, :], ALU.add).then_inc(S("z"), 1)
                v.wait_ge(S("z"), q.n + 1)
                settled(v)
                v.bn_stats(st[:, 0:6], zt).then_inc(S("z_stats"), 1)
                v.wait_ge(S("z_stats"), q.n + 1)
                v.tensor_tensor(st[:, 6:7], st[:, 1:2], st[:, 4:5], ALU.add)
                v.tensor_tensor(st[:, 7:8], st[:, 1:2], st[:, 4:5], ALU.subtract)
                v.tensor_tensor(st[:, 8:9], st[:, 2:3], st[:, 5:6], ALU.add).then_inc(S("z_sums"), 1)
                v.wait_ge(S("z_sums"), q.n + 1)
                v.tensor_scalar(st[:, 6:7], st[:, 6:7], 0.5, None, ALU.mult)
                v.scalar_tensor_tensor(st[:, 7:8], st[:, 7:8], 0.25, st[:, 7:8], ALU.mult, ALU.mult)
                v.tensor_scalar(st[:, 8:9], st[:, 8:9], 1.0 / D, LN_EPS, ALU.mult, ALU.add).then_inc(S("z_mean"), 1)
                v.wait_ge(S("z_mean"), q.n + 1)
                v.tensor_tensor(st[:, 8:9], st[:, 8:9], st[:, 7:8], ALU.add).then_inc(S("var_z"), 1)

            def x1_rows(q):
                v.wait_ge(S("std_z"), q.n + 1)
                v.reciprocal(st[:, 10:11], st[:, 9:10]).then_inc(S("z_inv"), 1)
                v.wait_ge(S("z_inv"), q.n + 1)
                v.tensor_tensor(st[:, 11:12], st[:, 10:11], st[:, 10:11], ALU.mult).then_inc(S("z_inv2"), 1)
                v.wait_ge(S("z_inv2"), q.n + 1)
                v.scalar_tensor_tensor(st[:, 12:13], st[:, 11:12], -0.5, st[:, 8:9], ALU.mult, ALU.mult).then_inc(S("z_newton"), 1)
                v.wait_ge(S("z_newton"), q.n + 1)
                v.scalar_tensor_tensor(st[:, 13:14], st[:, 12:13], 1.5, st[:, 10:11], ALU.add, ALU.mult).then_inc(S("z_rstd"), 1)
                v.wait_ge(S("z_rstd"), q.n + 1)
                if not q.first:
                    v.wait_ge(S("x1_stored"), q.n * 16)
                    v.wait_ge(S("x1_turned"), q.n)
                v.tensor_scalar(x1t, zt, st[:, 6:7], st[:, 13:14], ALU.subtract, ALU.mult).then_inc(S("x1_made"), 1)

            def pq_rows(q):
                v.wait_ge(S("pq_mm"), q.n + 1)
                if not q.first:
                    v.wait_ge(S("pq_stored"), q.n * 32)
                v.tensor_tensor(PQ, hp[1][0:R, 0:2 * D], q_bias[0:R, :], ALU.add).then_inc(S("pq_made"), 1)

            regs = [v.alloc_register(f"dve_base{k}") for k in range(U)]
            with v.If(general == 0):
                def body(t, base):
                    if due(t, Y0):
                        v.wait_ge(S("added0"), t.t - 3 if t.i is not None else min(t.static - 3, T))
                        y(due(t, Y0))
                    if t.back(3).within(T):
                        add(0, t.back(3), base)
                    if t.within(T):
                        for _ in onehot(0, t):
                            pass
                    if due(t, Y0 + 2):
                        z(due(t, Y0 + 2))
                    if due(t, Y0 + 3):
                        x1_rows(due(t, Y0 + 3))
                    if due(t, Y0 + 5):
                        pq_rows(due(t, Y0 + 5))
                turns(v, T, LAG0, body, top=lambda t: bases(v, regs, t.back(3)), peel=PEEL0)
                v.wait_ge(S("added0"), T)
            with v.Else():
                v.memset(fl[:, 0:1], 0.0).then_inc(S("g_summed0"), 1)
                with v.Fori(0, T) as t:
                    v.wait_ge(S("g_idx0"), (t + 1) * 32)
                    v.wait_ge(S("g_summed0"), t + 1)
                    add_wide(0, t)
                v.wait_ge(S("g_summed0"), T + 1)

                def body(q):
                    y(q)
                    z(q)
                    x1_rows(q)
                    pq_rows(q)
                tiles(v, body)
            v.wait_ge(S("sums_cleared"), NT)
            v.wait_ge(S("pq_stored"), 32 * NT)

            def newton_a(k, name):
                v.tensor_tensor(ra[:, k, :], r0[:, k, :], r0[:, k, :], ALU.mult)
                v.tensor_scalar(g1[:, k, :], ge[:, k, :], 1.0, None, ALU.add).then_inc(S(name), 1)

            def newton_b(k, name):
                v.scalar_tensor_tensor(rc[:, k, :], ss[:, k, :], float(D) * LN_EPS, ra[:, k, :], ALU.add, ALU.mult)
                v.reciprocal(gate[:, k, :], g1[:, k, :]).then_inc(S(name), 1)

            def newton_c(k, name):
                v.scalar_tensor_tensor(r1[:, k, :], rc[:, k, :], -3.0 * D, r0[:, k, :], ALU.add, ALU.mult).then_inc(S(name), 1)

            def scaled(k, name):
                for j in range(J):
                    a = v.scalar_tensor_tensor(msg[:, k, j, 0:D], h[:, k, j, :], r1[:, k, j:j + 1], g_bc[:, :], ALU.mult, ALU.mult)
                    if j == J - 1:
                        a.then_inc(S(name), 1)
                    yield

            def clipped(k, name):
                v.tensor_tensor(msg[:, k, :, 0:D], msg[:, k, :, 0:D], nb_bc[:, None, :].to_broadcast([P, J, D]), ALU.max).then_inc(S(name), 1)

            def add_rows(to, k, rows, part):
                lo, hi = ((0, 3), (3, J))[part]
                return v.tensor_tensor(h[:, k, lo:hi, :],
                                       to[:, HS[lo]:HS[lo] + (hi - lo) * (D + 1)].rearrange("p (j f) -> p j f", f=D + 1)[:, :, 0:D],
                                       rows[:, lo:hi, :], ALU.add)

            def clamp_rz(q):
                v.wait_ge(S("rz_mm"), q.n + 1)
                if not q.first:
                    v.wait_ge(S("z2_made"), q.n)
                v.tensor_scalar(rz, rz_ps, -40.0, None, ALU.max).then_inc(S("rz_clamped"), 1)

            def n_rows(q):
                v.wait_ge(S("n_mm"), q.n + 1)
                v.wait_ge(S("rz_made"), q.n + 1)
                if not q.first:
                    v.wait_ge(S("t1_made"), q.n)
                v.tensor_tensor(nn, rz[:, 0:D], n_ps[:, D:2 * D], ALU.mult).then_inc(S("rh"), 1)
                yield
                v.wait_ge(S("rh"), q.n + 1)
                v.tensor_tensor(nn, nn, n_ps[:, 0:D], ALU.add).then_inc(S("n_in"), 1)
                yield
                v.wait_ge(S("n_in"), q.n + 1)
                v.tensor_scalar(nn, nn, 20.0, None, ALU.min).then_inc(S("n_clamped"), 1)

            def z2_rows(q):
                v.wait_ge(S("n_made"), q.n + 1)
                v.wait_ge(S("xr1_loaded"), (q.n + 1) * 16)
                v.scalar_tensor_tensor(t1, nn, 2.0, xr1, ALU.mult, ALU.add).then_inc(S("t1_made"), 1)
                yield
                v.wait_ge(S("t1_made"), q.n + 1)
                v.scalar_tensor_tensor(zd, t1, -1.0, rz[:, D:2 * D], ALU.add, ALU.mult)
                v.scalar_tensor_tensor(z2t, xr1, 2.0, t1, ALU.mult, ALU.subtract).then_inc(S("zd_made"), 1)
                yield
                v.wait_ge(S("zd_made"), q.n + 1)
                v.scalar_tensor_tensor(z2t, z2t, 1.0, zd, ALU.add, ALU.add).then_inc(S("z2_made"), 1)
                yield
                v.wait_ge(S("z2_made"), q.n + 1)
                settled(v)
                v.bn_stats(sq1[:, 0:6], z2t).then_inc(S("z2_stats"), 1)
                yield
                v.wait_ge(S("z2_stats"), q.n + 1)
                v.tensor_tensor(sq1[:, 6:7], sq1[:, 1:2], sq1[:, 4:5], ALU.add)
                v.tensor_tensor(sq1[:, 7:8], sq1[:, 1:2], sq1[:, 4:5], ALU.subtract)
                v.tensor_tensor(sq1[:, 8:9], sq1[:, 2:3], sq1[:, 5:6], ALU.add).then_inc(S("z2_sums"), 1)
                yield
                v.wait_ge(S("z2_sums"), q.n + 1)
                v.tensor_scalar(sq1[:, 6:7], sq1[:, 6:7], 0.5, None, ALU.mult)
                v.scalar_tensor_tensor(sq1[:, 7:8], sq1[:, 7:8], 0.25, sq1[:, 7:8], ALU.mult, ALU.mult)
                v.tensor_scalar(sq1[:, 8:9], sq1[:, 8:9], 1.0 / D, LN_EPS, ALU.mult, ALU.add).then_inc(S("z2_mean"), 1)
                yield
                v.wait_ge(S("z2_mean"), q.n + 1)
                v.tensor_tensor(sq1[:, 8:9], sq1[:, 8:9], sq1[:, 7:8], ALU.add).then_inc(S("var_z2"), 1)

            def out_rows(q):
                v.wait_ge(S("z2_guess"), q.n + 1)
                v.tensor_tensor(sq1[:, 11:12], sq1[:, 10:11], sq1[:, 10:11], ALU.mult).then_inc(S("z2_inv2"), 1)
                yield
                v.wait_ge(S("z2_inv2"), q.n + 1)
                v.scalar_tensor_tensor(sq1[:, 12:13], sq1[:, 11:12], -0.5, sq1[:, 8:9], ALU.mult, ALU.mult).then_inc(S("z2_newton"), 1)
                yield
                v.wait_ge(S("z2_newton"), q.n + 1)
                v.scalar_tensor_tensor(sq1[:, 13:14], sq1[:, 12:13], 1.5, sq1[:, 10:11], ALU.add, ALU.mult).then_inc(S("z2_rstd"), 1)
                yield
                v.wait_ge(S("z2_rstd"), q.n + 1)
                if not q.first:
                    v.wait_ge(S("out_stored"), q.n * 16)
                v.tensor_scalar(ot, z2t, sq1[:, 6:7], sq1[:, 13:14], ALU.subtract, ALU.mult).then_inc(S("out_made"), 1)

            with v.If(general == 0):
                def body(t, base):
                    part = iter(())
                    if due(t, Y1 + 4):
                        part = n_rows(due(t, Y1 + 4))
                    if due(t, Y1 + 6):
                        part = z2_rows(due(t, Y1 + 6))
                    if due(t, Y1 + 9):
                        part = out_rows(due(t, Y1 + 9))
                    d, c, e = t.back(4), t.back(3), t.back(7)
                    first = onehot(1, t) if t.within(T) else iter(())
                    next(first, None)
                    if d.within(T):
                        k = d.slot % 2
                        v.wait_ge(S("r0_made"), d.t + 1)
                        newton_a(k, "newton_a")
                    if c.within(T):
                        v.wait_ge(S("ge_made"), c.t + 1)
                        v.wait_ge(S(f"gathered1_{c.slot}"), (c.lap + 1) * (16 * J))
                        add_rows(hp[c.slot % 2], c.slot % 2, Gx[:, c.slot], 0)
                    if d.within(T):
                        v.wait_ge(S("newton_a"), d.t + 1)
                        newton_b(k, "newton_b")
                    if c.within(T):
                        add_rows(hp[c.slot % 2], c.slot % 2, Gx[:, c.slot], 1).then_inc(S("h_added"), 1)
                    next(part, None)
                    if e.within(T):
                        add(1, e, base)
                    if d.within(T):
                        v.wait_ge(S("newton_b"), d.t + 1)
                        newton_c(k, "newton_c")
                        if d.since(2):
                            v.wait_ge(S("sums_made1"), d.t - 1)
                        v.tensor_tensor(Sg[:, k], Ce[:, d.slot, :, ED:C], gate[:, k, :, None].to_broadcast([P, J, W]),
                                        ALU.mult).then_inc(S("Sg_made"), 1)
                    next(part, None)
                    rows = iter(())
                    if d.within(T):
                        v.wait_ge(S("newton_c"), d.t + 1)
                        rows = scaled(k, "scaled")
                    next(rows, None)
                    next(part, None)
                    for _ in first:
                        pass
                    for _ in rows:
                        next(part, None)
                    for _ in part:
                        pass
                    if due(t, Y1 + 2):
                        if t.back(1).within(T):
                            v.wait_ge(S("tile_copied"), t.t)
                        clamp_rz(due(t, Y1 + 2))
                    if d.within(T):
                        v.wait_ge(S("scaled"), d.t + 1)
                        clipped(k, "msg_made")
                turns(v, T, LAG1, body, top=lambda t: bases(v, regs, t.back(7)), peel=PEEL1)
            with v.Else():
                v.memset(fl[:, 0:1], 0.0).then_inc(S("g_summed1"), 1)
                with v.Fori(0, T) as t:
                    v.wait_ge(S("h_made"), t + 1)
                    v.wait_ge(S("ge_made"), t + 1)
                    v.wait_ge(S("g_gathered1"), (t + 1) * (32 * J))
                    v.wait_ge(S("g_summed1"), t + 1)
                    add_rows(hp[0], 0, Gx[:, 0], 0)
                    add_rows(hp[0], 0, Gx[:, 0], 1).then_inc(S("g_rows"), 1)
                    v.wait_ge(S("g_rows"), t + 1)
                    v.tensor_tensor(h[:, 0], h[:, 0], Gx[:, 1], ALU.add).then_inc(S("h_added"), 1)
                    v.wait_ge(S("r0_made"), t + 1)
                    newton_a(0, "newton_a")
                    v.wait_ge(S("newton_a"), t + 1)
                    newton_b(0, "newton_b")
                    v.wait_ge(S("newton_b"), t + 1)
                    newton_c(0, "newton_c")
                    v.wait_ge(S("newton_c"), t + 1)
                    for _ in scaled(0, "scaled"):
                        pass
                    v.wait_ge(S("scaled"), t + 1)
                    clipped(0, "msg_made")
                    v.wait_ge(S("msg_made"), t + 1)
                    add_wide(1, t)
                v.wait_ge(S("g_summed1"), T + 1)

                def body(q):
                    clamp_rz(q)
                    for part in (n_rows, z2_rows, out_rows):
                        for _ in part(q):
                            pass
                tiles(v, body)


_INS = ['x', 'src', 'dst', 'edge_attr_64', 'L0_gnn_eps', 'L0_gnn_W1', 'L0_gnn_b1', 'L0_gnn_W2', 'L0_gnn_b2',
        'L1_gnn_W1', 'L1_gnn_b1', 'L1_gnn_ln_g', 'L1_gnn_ln_b', 'L1_gnn_W2', 'L1_gnn_b2', 'L1_gnn_gate_w',
        'L1_gnn_gate_b', 'L1_gnn_W_ih', 'L1_gnn_b_ih', 'L1_gnn_W_hh', 'L1_gnn_b_hh']


def kernel(**inputs):
    import numpy as _np
    import concourse.bacc as _bacc
    from concourse import mybir as _mybir
    from concourse.bass_utils import run_bass_kernel_spmd as _run

    nc = _bacc.Bacc("TRN2", target_bir_lowering=False, num_devices=1)
    arrays, args = {}, []
    for name in _INS:
        a = _np.ascontiguousarray(inputs[name])
        arrays[f"in_{name}_dram"] = a
        args.append(nc.dram_tensor(f"in_{name}_dram", a.shape, _mybir.dt.from_np(a.dtype), kind="ExternalInput").ap())
    o = nc.dram_tensor("out_0_dram", inputs['x'].shape, _mybir.dt.float32, kind="ExternalOutput").ap()
    bass_gnn_kernel(nc, *args, o)
    r = _run(nc, [arrays], core_ids=[0])
    return r.results[0]["out_0_dram"]
```
